# Optimizing a Trainium2 kernel written in Bass

```python
import numpy as np
import jax
import jax.numpy as jnp

def _softmax(x, axis=-1):
    return jax.nn.softmax(x, axis=axis)

def _gelu(x):
    return jax.nn.gelu(x, approximate=True)

def _silu(x):
    return jax.nn.silu(x)

def _sigmoid(x):
    return jax.nn.sigmoid(x)

def _layernorm(x, axis=-1, eps=1e-05):
    m = jnp.mean(x, axis=axis, keepdims=True)
    v = jnp.var(x, axis=axis, keepdims=True)
    return (x - m) / jnp.sqrt(v + eps)

def _scatter_add(tgt, idx, src, axis=0):
    return tgt.at[idx].add(src)

def _segment_sum(src, seg, n):
    return jax.ops.segment_sum(src, seg, n)
kernel_name = 'mk_gnn_resnorm_d2_gnn_r8_24da74'

def setup_inputs(seed: int=0):
    np.random.seed(seed)
    _w = jnp.asarray

    def _rec_inputs():
        import jax
        import jax.numpy as jnp
        _gk = jax.random.key(seed)
        x = -0.000202 + 1 * jax.random.normal(jax.random.fold_in(_gk, 1), (6250, 128), jnp.float32)
        _s = jax.random.randint(jax.random.fold_in(_gk, 2), (100000,), 0, 6250, jnp.int32)
        _d = jax.random.randint(jax.random.fold_in(_gk, 3), (100000,), 0, 6250, jnp.int32)
        _loop = jnp.arange(6250, dtype=jnp.int32)
        src = jnp.concatenate([_s, _d, _loop])
        dst = jnp.concatenate([_d, _s, _loop])
        _o = jnp.argsort(dst, stable=True)
        src = src[_o]
        dst = dst[_o]
        edge_type_5 = jax.random.randint(jax.random.fold_in(_gk, 12), (206250,), 0, 5, jnp.int32)
        node_type_3 = jax.random.randint(jax.random.fold_in(_gk, 13), (6250,), 0, 3, jnp.int32)
        return (x, src, dst, edge_type_5, node_type_3)
    x, src, dst, edge_type_5, node_type_3 = _rec_inputs()

    def _L0_gnn_setup():
        import jax, jax.numpy as jnp
        import numpy as np
        N_NODES = 6250
        N_EDGES = 75000
        HIDDEN = 128

        def _sage_conv(x, src, dst, Wl, bl, Wr):
            msg_sum = jax.ops.segment_sum(x[src], dst, num_segments=N_NODES)
            deg = jax.ops.segment_sum(jnp.ones((src.shape[0],), x.dtype), dst, num_segments=N_NODES)
            agg = msg_sum / jnp.maximum(deg, 1.0)[:, None]
            return agg @ Wl.T + bl + x @ Wr.T
        key = jax.random.key(seed)
        ks = jax.random.split(key, 8)
        x = jax.random.normal(ks[0], (N_NODES, HIDDEN), dtype=jnp.float32)
        edge_index = jax.random.randint(ks[1], (2, N_EDGES), 0, N_NODES, dtype=jnp.int32)
        s = 1.0 / np.sqrt(HIDDEN)
        W1l = jax.random.uniform(ks[2], (HIDDEN, HIDDEN), jnp.float32, -s, s)
        b1l = jax.random.uniform(ks[3], (HIDDEN,), jnp.float32, -s, s)
        W1r = jax.random.uniform(ks[4], (HIDDEN, HIDDEN), jnp.float32, -s, s)
        W2l = jax.random.uniform(ks[5], (HIDDEN, HIDDEN), jnp.float32, -s, s)
        b2l = jax.random.uniform(ks[6], (HIDDEN,), jnp.float32, -s, s)
        W2r = jax.random.uniform(ks[7], (HIDDEN, HIDDEN), jnp.float32, -s, s)
        return {'x': x, 'edge_index': edge_index, 'W1l': W1l, 'b1l': b1l, 'W1r': W1r, 'W2l': W2l, 'b2l': b2l, 'W2r': W2r}
    _L0_gnn_all = _L0_gnn_setup()
    _L0_gnn_in = {k: v for k, v in _L0_gnn_all.items() if k in ('W1l', 'b1l', 'W1r', 'W2l', 'b2l', 'W2r')}
    del _L0_gnn_all

    def _L1_gnn_setup():
        import jax, jax.numpy as jnp
        import numpy as np
        N = 6250
        E = 125000
        R = 5
        IN = 128
        TD = 128
        H = 128
        OUT = 128
        NT = 3
        D0 = IN + TD

        def rgcn_conv(x, src, dst, etype, W, root, bias):
            n = x.shape[0]
            seg = dst * R + etype
            x_src = x[src]
            agg = jax.ops.segment_sum(x_src, seg, num_segments=n * R)
            cnt = jax.ops.segment_sum(jnp.ones((src.shape[0],), x.dtype), seg, num_segments=n * R)
            agg = jnp.where(cnt[:, None] > 0, agg / jnp.maximum(cnt, 1.0)[:, None], 0.0)
            agg = agg.reshape(n, R, -1)
            return jnp.einsum('nrd,rdk->nk', agg, W) + x @ root + bias
        key = jax.random.key(seed)
        ks = jax.random.split(key, 16)
        s = 0.05
        return {'x': jax.random.normal(ks[0], (N, IN), jnp.float32), 'node_type': jax.random.randint(ks[1], (N,), 0, NT), 'edge_index': jax.random.randint(ks[2], (2, E), 0, N), 'edge_type': jax.random.randint(ks[3], (E,), 0, R), 'node_emb': jax.random.normal(ks[4], (NT, TD), jnp.float32) * s, 'W1': jax.random.normal(ks[5], (R, D0, D0), jnp.float32) * s, 'root1': jax.random.normal(ks[6], (D0, D0), jnp.float32) * s, 'b1': jnp.zeros((D0,), jnp.float32), 'W2': jax.random.normal(ks[7], (R, D0, H), jnp.float32) * s, 'root2': jax.random.normal(ks[8], (D0, H), jnp.float32) * s, 'b2': jnp.zeros((H,), jnp.float32), 'W3': jax.random.normal(ks[9], (R, H, OUT), jnp.float32) * s, 'root3': jax.random.normal(ks[10], (H, OUT), jnp.float32) * s, 'b3': jnp.zeros((OUT,), jnp.float32)}
    _L1_gnn_all = _L1_gnn_setup()
    _L1_gnn_in = {k: v for k, v in _L1_gnn_all.items() if k in ('node_emb', 'W1', 'root1', 'b1', 'W2', 'root2', 'b2', 'W3', 'root3', 'b3')}
    del _L1_gnn_all
    return {'x': x, 'src': src, 'dst': dst, 'edge_type_5': edge_type_5, 'node_type_3': node_type_3, 'L0_gnn_W1l': _L0_gnn_in['W1l'], 'L0_gnn_b1l': _L0_gnn_in['b1l'], 'L0_gnn_W1r': _L0_gnn_in['W1r'], 'L0_gnn_W2l': _L0_gnn_in['W2l'], 'L0_gnn_b2l': _L0_gnn_in['b2l'], 'L0_gnn_W2r': _L0_gnn_in['W2r'], 'L1_gnn_node_emb': _L1_gnn_in['node_emb'], 'L1_gnn_W1': _L1_gnn_in['W1'], 'L1_gnn_root1': _L1_gnn_in['root1'], 'L1_gnn_b1': _L1_gnn_in['b1'], 'L1_gnn_W2': _L1_gnn_in['W2'], 'L1_gnn_root2': _L1_gnn_in['root2'], 'L1_gnn_b2': _L1_gnn_in['b2'], 'L1_gnn_W3': _L1_gnn_in['W3'], 'L1_gnn_root3': _L1_gnn_in['root3'], 'L1_gnn_b3': _L1_gnn_in['b3']}

def reference(x, src, dst, edge_type_5, node_type_3, L0_gnn_W1l, L0_gnn_b1l, L0_gnn_W1r, L0_gnn_W2l, L0_gnn_b2l, L0_gnn_W2r, L1_gnn_node_emb, L1_gnn_W1, L1_gnn_root1, L1_gnn_b1, L1_gnn_W2, L1_gnn_root2, L1_gnn_b2, L1_gnn_W3, L1_gnn_root3, L1_gnn_b3):
    import jax
    import jax.numpy as jnp

    def _L0_gnn_ref(x, edge_index, W1l, b1l, W1r, W2l, b2l, W2r):
        import jax, jax.numpy as jnp
        import numpy as np
        N_NODES = 6250
        N_EDGES = 75000
        HIDDEN = 128

        def _sage_conv(x, src, dst, Wl, bl, Wr):
            msg_sum = jax.ops.segment_sum(x[src], dst, num_segments=N_NODES)
            deg = jax.ops.segment_sum(jnp.ones((src.shape[0],), x.dtype), dst, num_segments=N_NODES)
            agg = msg_sum / jnp.maximum(deg, 1.0)[:, None]
            return agg @ Wl.T + bl + x @ Wr.T
        src, dst = (edge_index[0], edge_index[1])
        h = jax.nn.relu(_sage_conv(x, src, dst, W1l, b1l, W1r))
        out = _sage_conv(h, src, dst, W2l, b2l, W2r)
        return out

    def _L1_gnn_ref(x, node_type, edge_index, edge_type, node_emb, W1, root1, b1, W2, root2, b2, W3, root3, b3):
        import jax, jax.numpy as jnp
        import numpy as np
        N = 6250
        E = 125000
        R = 5
        IN = 128
        TD = 128
        H = 128
        OUT = 128
        NT = 3
        D0 = IN + TD

        def rgcn_conv(x, src, dst, etype, W, root, bias):
            n = x.shape[0]
            seg = dst * R + etype
            x_src = x[src]
            agg = jax.ops.segment_sum(x_src, seg, num_segments=n * R)
            cnt = jax.ops.segment_sum(jnp.ones((src.shape[0],), x.dtype), seg, num_segments=n * R)
            agg = jnp.where(cnt[:, None] > 0, agg / jnp.maximum(cnt, 1.0)[:, None], 0.0)
            agg = agg.reshape(n, R, -1)
            return jnp.einsum('nrd,rdk->nk', agg, W) + x @ root + bias
        src, dst = (edge_index[0], edge_index[1])
        h = jnp.concatenate([x, node_emb[node_type]], axis=-1)
        h = jax.nn.relu(rgcn_conv(h, src, dst, edge_type, W1, root1, b1))
        h = jax.nn.relu(rgcn_conv(h, src, dst, edge_type, W2, root2, b2))
        h = rgcn_conv(h, src, dst, edge_type, W3, root3, b3)
        return jax.nn.relu(h)
    edge_index = jnp.stack([src, dst])
    x = _layernorm(x + _L0_gnn_ref(x, edge_index, L0_gnn_W1l, L0_gnn_b1l, L0_gnn_W1r, L0_gnn_W2l, L0_gnn_b2l, L0_gnn_W2r), axis=-1)
    x = _layernorm(x + _L1_gnn_ref(x, node_type_3, edge_index, edge_type_5, L1_gnn_node_emb, L1_gnn_W1, L1_gnn_root1, L1_gnn_b1, L1_gnn_W2, L1_gnn_root2, L1_gnn_b2, L1_gnn_W3, L1_gnn_root3, L1_gnn_b3), axis=-1)
    return x

_drawn_inputs = setup_inputs


def setup_inputs(seed=0):
    import zlib

    import numpy as np

    out = dict(_drawn_inputs(seed))
    spreads = {'L1_gnn_b1': (0.0, 0.1), 'L1_gnn_b2': (0.0, 0.1), 'L1_gnn_b3': (0.0, 0.1)}
    factors = {}
    for name, (base, spread) in spreads.items():
        noise = np.random.default_rng([zlib.crc32(name.encode()), seed]).standard_normal(out[name].shape)
        drawn = base * np.exp(spread * noise) if base else spread * noise
        out[name] = jnp.asarray(drawn.astype(out[name].dtype))
    for name, factor in factors.items():
        out[name] = (out[name] * factor).astype(out[name].dtype)
    return out
```

```python
from contextlib import ExitStack

import concourse.bass as bass
from concourse import mybir

P = 128
N_NODES = 6250
N_EDGES = 206250
FEAT = 128
WIDE = 256
RELATIONS = 5
NODE_TYPES = 3
EPS = 1e-5

NODE_TILES = -(-N_NODES // P)
NODES_PADDED = NODE_TILES * P
CHUNKS = 7
TILES_PER_CHUNK = NODE_TILES // CHUNKS
HALF = TILES_PER_CHUNK * P // 2
ACC_COLS = NODES_PADDED + P

EDGE_TILES = -(-N_EDGES // P)
GROUP = 13
GROUPS = EDGE_TILES // GROUP
assert GROUPS * GROUP == EDGE_TILES and GROUPS % 2 == 0
PAIRS = GROUPS // 2
EDGE_BLOCKS = -(-EDGE_TILES // P)
FULL_BLOCKS = EDGE_TILES // P
LAST_ROWS = N_EDGES // P - FULL_BLOCKS * P
LAST_NODES = N_NODES - (NODE_TILES - 1) * P
LAST_EDGES = N_EDGES % P
NO_NODE = 1000000

CONV_WIDTH = [FEAT, FEAT, WIDE, FEAT, FEAT]
CONVS = len(CONV_WIDTH)


def resnorm_gnn(nc, a, out):
    f32, i32 = mybir.dt.float32, mybir.dt.int32
    ALU, ACT, AX = mybir.AluOpType, mybir.ActivationFunctionType, mybir.AxisListType
    ds = bass.ds

    table_h = nc.dram_tensor("table_h", (NODES_PADDED, FEAT), f32).ap()
    table_1 = nc.dram_tensor("table_1", (NODES_PADDED, RELATIONS * WIDE), f32).ap()
    table_2 = nc.dram_tensor("table_2", (NODES_PADDED, RELATIONS * FEAT), f32).ap()
    table_3 = nc.dram_tensor("table_3", (NODES_PADDED, RELATIONS * FEAT), f32).ap()
    per_relation = lambda t: t.rearrange("n (r f) -> (n r) f", r=RELATIONS)
    GATHERED = [a["x"], table_h, per_relation(table_1), per_relation(table_2), per_relation(table_3)]
    STORED = [table_h, table_1, table_2, table_3]
    bounds_d = nc.dram_tensor("bounds_d", (2, EDGE_BLOCKS * P), f32).ap()
    types_d = nc.dram_tensor("types_d", (1, EDGE_TILES * P), i32).ap()

    ctx = ExitStack()
    with ctx:
        sb = lambda name, shape, dt=f32: ctx.enter_context(nc.sbuf_tensor(name, shape, dt))
        sem = lambda name: ctx.enter_context(nc.semaphore(name))

        S = [sb(f"S{n}", [P, ACC_COLS]) for n in range(4)]
        SUMMED, INVERSE, COUNT, NTYPE = slice(0, 32), slice(0, RELATIONS), slice(32, 64), slice(64, 64 + NODE_TYPES)
        msgs = sb("msgs", [P, 2 * GROUP * WIDE])
        onehot = sb("onehot", [P, GROUP, P])
        row_all = sb("row_all", [P, EDGE_TILES], i32)
        rel_row_all = sb("rel_row_all", [P, EDGE_TILES], i32)
        rel_all = sb("rel_all", [P, EDGE_TILES])
        type_all = sb("type_all", [P, EDGE_TILES])
        weight_all = sb("weight_all", [P, EDGE_TILES])
        row_cur = sb("row_cur", [P, 2, GROUP], i32)
        rel_cur = sb("rel_cur", [P, 2, GROUP])
        weight_cur = sb("weight_cur", [P, 2, GROUP])
        rel_wide = sb("rel_wide", [P, GROUP])
        typehot = sb("typehot", [P, GROUP, 32])
        part = sb("part", [P, GROUP])
        part_wide = sb("part_wide", [P, GROUP])
        base_f = sb("base_f", [P, GROUPS])
        high_f = sb("high_f", [P, GROUPS])
        span_f = sb("span_f", [P, GROUPS])
        wide_f = sb("wide_f", [P, 1])
        narrow_f = sb("narrow_f", [P, 1])
        base_i = sb("base_i", [1, GROUPS], i32)
        wide_i = sb("wide_i", [1, 1], i32)
        tile_low = sb("tile_low", [P, EDGE_BLOCKS])
        tile_high = sb("tile_high", [P, EDGE_BLOCKS])
        iota_i = sb("iota_i", [P, P], i32)
        iota_f = sb("iota_f", [P, P])
        lane_i = sb("lane_i", [P, 2], i32)
        lane_f = sb("lane_f", [P, 2])
        ident = sb("ident", [P, P])
        ones = sb("ones", [P, P])
        eps = sb("eps", [P, 1])
        bias = sb("bias", [P, 6])
        w_T = sb("w_T", [P, 4, P])
        emb = sb("emb", [P, FEAT])
        table_w = sb("table_w", [P, 2 * RELATIONS * WIDE])
        root1 = sb("root1", [P, 2, WIDE])
        root2 = sb("root2", [P, 2, FEAT])
        root3 = sb("root3", [P, FEAT])
        chunk_in = sb("chunk_in", [P, 2, 2 * HALF])
        inv_deg = sb("inv_deg", [P, 2, HALF])
        stats = sb("stats", [P, TILES_PER_CHUNK, 6])
        moments = sb("moments", [P, TILES_PER_CHUNK, 2])
        rstd = sb("rstd", [P, TILES_PER_CHUNK])
        normed = sb("normed", [P, TILES_PER_CHUNK, P])
        etype_row_t = sb("etype_row", [P, GROUP * P], i32)

        bank = [ctx.enter_context(nc.psum_tensor(f"bank{n}", [P, 512], f32)) for n in range(8)]

        x_tiles = msgs[:, 0:NODE_TILES * P].rearrange("p (t f) -> p t f", f=P)
        edge_cols = EDGE_BLOCKS * P
        edge_f = [S[2][:, n * edge_cols:(n + 1) * edge_cols].rearrange("p (b c) -> p b c", c=P) for n in range(3)]
        edge_i = [v.bitcast(i32) for v in edge_f]
        src_T = S[1][:, 0:edge_cols]
        dst_T = S[1][:, edge_cols:2 * edge_cols]
        ntype_i = S[3][NTYPE, 0:N_NODES].bitcast(i32)
        etype_row = etype_row_t[INVERSE, :]
        w_raw = etype_row_t[:, 0:4 * P].bitcast(f32).rearrange("p (n f) -> p n f", n=4)
        etype_hot = msgs[INVERSE, 2 * GROUP * FEAT:2 * GROUP * FEAT + GROUP * P]
        bounds = onehot[:, :, :].rearrange("p k c -> p (k c)")
        stage = msgs[:, 0:2 * RELATIONS * WIDE].rearrange("p (s f) -> p s f", s=2)

        def message(conv, half, k, f):
            w = CONV_WIDTH[conv]
            at = (half * GROUP + k) * w
            return msgs[:, at + f * P:at + (f + 1) * P]

        def message_row(conv, half, k):
            w = CONV_WIDTH[conv]
            at = (half * GROUP + k) * w
            return msgs[:, at:at + w]

        SUMS = [[S[1]], [S[2]], [S[2], S[3]], [S[1]], [S[2]]]

        UPDATE = [
            [[(w_T[:, 0, :], S[1]), (w_T[:, 1, :], S[0])]],
            [[(w_T[:, 3, :], S[1])]],
            [[(root1[:, 0, f * P:(f + 1) * P], S[0]), (root1[:, 1, f * P:(f + 1) * P], S[1])] for f in range(2)],
            [[(root2[:, 0, :], S[2]), (root2[:, 1, :], S[3])]],
            [[(root3[:, :], S[1])]],
        ]
        BIAS = [[bias[:, 0:1]], [bias[:, 1:2]], [bias[:, 2:3], bias[:, 3:4]], [bias[:, 4:5]], [bias[:, 5:6]]]
        TABLE_IN = [[S[1]], [S[0], S[1]], [S[2], S[3]], [S[1]]]
        TABLE_COLS = [FEAT, RELATIONS * WIDE, RELATIONS * FEAT, RELATIONS * FEAT]

        def table_weights(p, h, at, n):
            return w_T[:, 2, :] if p == 0 else table_w[:, h * TABLE_COLS[p] + at:h * TABLE_COLS[p] + at + n]

        cuts = lambda n: [(c, min(512, n - c)) for c in range(0, n, 512)]
        node_cols = lambda c, u: ds(c * (TILES_PER_CHUNK * P) + u * HALF, HALF)
        node_cols2 = lambda c: ds(c * (TILES_PER_CHUNK * P), TILES_PER_CHUNK * P)
        chunk_copies = lambda p: 4 if p == 1 else len(TABLE_IN[p])
        tile_cols = lambda c, t, n=1: ds(c * (TILES_PER_CHUNK * P) + t * P, n * P)
        NORM_CUTS = [(0, 4), (4, 3)]

        padded, edges_in, types_padded, x_in, w_in = sem("padded"), sem("edges_in"), sem("types_padded"), sem("x_in"), sem("w_in")
        bounds_out, bounds_in = sem("bounds_out"), sem("bounds_in")
        table_w_in = sem("table_w_in")
        consts = sem("consts")
        vec_prep = sem("vec_prep")
        prep_psum, prep_kept = sem("prep_psum"), sem("prep_kept")
        inverted = sem("inverted")
        zeroed = sem("zeroed")
        cursor_free, cursor_ready = sem("cursor_free"), sem("cursor_ready")
        gathers_begun, moments_begun = sem("gathers_begun"), sem("moments_begun")
        gathered = [[sem(f"gathered{h}_{k}") for k in range(GROUP)] for h in range(2)]
        onehot_ready, sums_psum = sem("onehot_ready"), sem("sums_psum")
        etype_in, etype_hot_ready = sem("etype_in"), sem("etype_hot_ready")
        lookup_psum, looked_up = sem("lookup_psum"), sem("looked_up")
        wide_onehot, wide_psum, wide_rel, wide_part = sem("wide_onehot"), sem("wide_psum"), sem("wide_rel"), sem("wide_part")
        deg_psum, deg_step, scaled = sem("deg_psum"), sem("deg_step"), sem("scaled")
        update_psum = [sem(f"update_psum{p}") for p in range(CONVS)]
        update_step = [sem(f"update_step{p}") for p in range(CONVS)]
        updated = [sem(f"updated{p}") for p in range(CONVS)]
        counts_kept = sem("counts_kept")
        chunk_kept = [sem(f"chunk_kept{p}") for p in range(4)]
        turned, deviation, norm_step, normed_ready = sem("turned"), sem("deviation"), sem("norm_step"), sem("normed_ready")
        turned_back, norm_kept = sem("turned_back"), sem("norm_kept")
        emb_psum, emb_kept = sem("emb_psum"), sem("emb_kept")
        table_psum = [sem(f"table_psum{p}") for p in range(4)]
        table_copied = [sem(f"table_copied{p}") for p in range(4)]
        row_stored = [[sem(f"row_stored{p}_{s}") for s in range(2)] for p in range(4)]
        out_stored = sem("out_stored")

        CURSORS = 3
        freed = lambda conv: 2 + GROUPS * (conv + 1)
        slot_stores = lambda s: (TILES_PER_CHUNK + 1 - s) // 2
        tile_copies = lambda p: len(cuts(TABLE_COLS[p]))
        VEC_PREPARED = 22
        FILLS = [("w", 0, 4)]
        FILLS += [(n, b, min(4, EDGE_BLOCKS - b)) for n in range(3) for b in range(0, EDGE_BLOCKS, 4)]
        EDGE_FILLS = len(FILLS)
        FILLS += [("x", t, min(4, NODE_TILES - t)) for t in range(0, NODE_TILES, 4)]

        with nc.Block() as block:

            @block.sync
            def _(sp):
                sp.wait_ge(padded, 5)
                full = FULL_BLOCKS * P * P
                whole = full + LAST_ROWS * P
                for n, name in enumerate(["dst", "src", "edge_type_5"]):
                    e = a[name]
                    sp.dma_start(edge_i[n][:, 0:FULL_BLOCKS, :], e[0:full].rearrange("(b r c) -> r b c", r=P, c=P)).then_inc(edges_in, 16)
                    sp.dma_start(edge_i[n][0:LAST_ROWS, FULL_BLOCKS, :], e[full:whole].rearrange("(r c) -> r c", c=P)).then_inc(edges_in, 16)
                    sp.dma_start(edge_i[n][LAST_ROWS:LAST_ROWS + 1, FULL_BLOCKS, 0:LAST_EDGES], e[whole:N_EDGES].rearrange("(o c) -> o c", o=1)).then_inc(edges_in, 16)
                sp.dma_start(ntype_i, a["node_type_3"].rearrange("(o n) -> o n", o=1).broadcast_to([NODE_TYPES, N_NODES])).then_inc(edges_in, 16)
                for n, name in enumerate(["L0_gnn_W1l", "L0_gnn_W1r", "L0_gnn_W2l", "L0_gnn_W2r"]):
                    sp.dma_start(w_raw[:, n, :], a[name]).then_inc(w_in, 16)
                with sp.Fori(0, NODE_TILES - 1) as t:
                    sp.dma_start(msgs[:, ds(t * P, P)], a["x"][ds(t * P, P), :]).then_inc(x_in, 16)
                sp.dma_start(x_tiles[0:LAST_NODES, NODE_TILES - 1, :], a["x"][(NODE_TILES - 1) * P:N_NODES, :]).then_inc(x_in, 16)
                for n, name in enumerate(["L0_gnn_b1l", "L0_gnn_b2l"]):
                    sp.dma_start(bias[:, n:n + 1], a[name].rearrange("(p o) -> p o", o=1)).then_inc(w_in, 16)
                for f in range(2):
                    sp.dma_start(bias[:, 2 + f:3 + f], a["L1_gnn_b1"][f * P:(f + 1) * P].rearrange("(p o) -> p o", o=1)).then_inc(w_in, 16)
                for n, name in enumerate(["L1_gnn_b2", "L1_gnn_b3"]):
                    sp.dma_start(bias[:, 4 + n:5 + n], a[name].rearrange("(p o) -> p o", o=1)).then_inc(w_in, 16)
                sp.dma_start(emb[NTYPE, :], a["L1_gnn_node_emb"]).then_inc(w_in, 16)
                sp.dma_start(root1[:, :, :], a["L1_gnn_root1"].rearrange("(h p) o -> p h o", p=P)).then_inc(w_in, 16)
                sp.dma_start(root2[:, :, :], a["L1_gnn_root2"].rearrange("(h p) o -> p h o", p=P)).then_inc(w_in, 16)
                sp.dma_start(root3[:, :], a["L1_gnn_root3"]).then_inc(w_in, 16)

                def load_table_weights(p, name):
                    n = TABLE_COLS[p]
                    for h in range(len(TABLE_IN[p])):
                        sp.dma_start(table_w[:, h * n:(h + 1) * n].rearrange("p (r o) -> p r o", r=RELATIONS),
                                     a[name][:, h * P:(h + 1) * P, :].rearrange("r p o -> p r o")).then_inc(table_w_in, 16)

                load_table_weights(1, "L1_gnn_W1")
                sp.dma_start(types_d[0, 0:N_EDGES].rearrange("(r c) -> r c", c=1650), a["edge_type_5"].rearrange("(r c) -> r c", c=1650)).then_inc(types_padded, 16)
                sp.wait_ge(edges_in, 160)
                sp.dma_start(types_d[0:1, N_EDGES:EDGE_TILES * P], edge_i[2][LAST_ROWS:LAST_ROWS + 1, FULL_BLOCKS, LAST_EDGES:P]).then_inc(types_padded, 16)
                sp.wait_ge(vec_prep, 10)
                for n, t in enumerate([tile_low, tile_high]):
                    sp.dma_start(bounds_d[n, :].rearrange("(b r) -> r b", r=P), t[:, :], allow_slow_non_contiguous=True).then_inc(bounds_out, 16)
                sp.wait_ge(bounds_out, 32)
                sp.dma_start(bounds, bounds_d[0:1, :].broadcast_to([P, edge_cols])).then_inc(bounds_in, 16)
                sp.wait_ge(vec_prep, 11)
                sp.dma_start(bounds, bounds_d[1:2, :].broadcast_to([P, edge_cols])).then_inc(bounds_in, 16)

                def store_table(p):
                    copies = tile_copies(p)
                    with sp.Fori(0, CHUNKS) as c:
                        for t in range(TILES_PER_CHUNK):
                            sp.wait_ge(table_copied[p], c * (TILES_PER_CHUNK * copies) + (t + 1) * copies)
                            sp.dma_start(STORED[p][tile_cols(c, t), :], stage[:, t % 2, 0:TABLE_COLS[p]]).then_inc(row_stored[p][t % 2], 16)

                store_table(0)
                sp.wait_ge(types_padded, 32)
                with sp.Fori(0, GROUPS) as g:
                    sp.wait_ge(etype_hot_ready, g)
                    sp.dma_start(etype_row, types_d[0:1, ds(g * (GROUP * P), GROUP * P)].broadcast_to([RELATIONS, GROUP * P])).then_inc(etype_in, 16)
                store_table(1)
                load_table_weights(2, "L1_gnn_W2")
                store_table(2)
                load_table_weights(3, "L1_gnn_W3")
                store_table(3)

                def store_out(c):
                    sp.wait_ge(normed_ready, CHUNKS + c + 1)
                    last = isinstance(c, int) and c == CHUNKS - 1
                    whole_tiles = TILES_PER_CHUNK - 1 if last else TILES_PER_CHUNK
                    sp.dma_start(out[ds(c * (TILES_PER_CHUNK * P), whole_tiles * P), :].rearrange("(t p) f -> p t f", p=P), normed[:, 0:whole_tiles, :]).then_inc(out_stored, 16)
                    if last:
                        sp.dma_start(out[(NODE_TILES - 1) * P:N_NODES, :], normed[0:LAST_NODES, whole_tiles, :]).then_inc(out_stored, 16)

                with sp.Fori(0, CHUNKS - 1) as c:
                    store_out(c)
                store_out(CHUNKS - 1)
                sp.wait_ge(out_stored, 16 * (CHUNKS + 1))

            @block.gpsimd
            def _(pool):
                pool.memset(edge_i[0][:, FULL_BLOCKS, :], NO_NODE).then_inc(padded, 1)
                pool.memset(edge_i[1][:, FULL_BLOCKS, :], 0).then_inc(padded, 1)
                pool.memset(edge_i[2][:, FULL_BLOCKS, :], 0).then_inc(padded, 1)
                pool.memset(x_tiles[:, NODE_TILES - 1, :], 0.0).then_inc(padded, 1)
                pool.memset(S[3][:, :], 0.0).then_inc(padded, 1)
                pool.iota(iota_i[:, :], [[1, P]], base=0, channel_multiplier=0).then_inc(consts, 1)
                for n, start in enumerate([0, NTYPE.start]):
                    pool.iota(lane_i[:, n:n + 1], [[0, 1]], base=-start, channel_multiplier=1).then_inc(consts, 1)
                pool.memset(ones[:, :], 1.0).then_inc(consts, 1)
                pool.memset(eps[:, :], EPS).then_inc(consts, 1)
                pool.wait_ge(prep_kept, len(FILLS))

                for conv in range(CONVS):
                    width = CONV_WIDTH[conv]
                    if conv:
                        for s in range(2):
                            pool.wait_ge(row_stored[conv - 1][s], 16 * CHUNKS * slot_stores(s))
                    with pool.Fori(0, PAIRS) as i:
                        for half in range(2):
                            pool.wait_ge(cursor_ready, CURSORS * GROUPS * conv + i * (2 * CURSORS) + CURSORS * (half + 1))
                            pool.sem_inc(gathers_begun, 1)
                            for k in range(GROUP):
                                at = (half * GROUP + k) * width
                                pool.indirect_dma_start(
                                    msgs[:, at:at + width], None, GATHERED[conv],
                                    bass.IndirectOffsetOnAxis(ap=row_cur[:, half, k:k + 1], axis=0),
                                ).then_inc(gathered[half][k], 16)

            @block.scalar
            def _(act):
                for n, (what, at, count) in enumerate(FILLS):
                    if n == EDGE_FILLS:
                        act.wait_ge(padded, 5)
                    act.wait_ge(prep_psum, n + 1)
                    src = bank[n % 8][:, 0:count * P]
                    if what == "w":
                        to = w_T[:, :, :].rearrange("p n f -> p (n f)")
                    elif what == "x":
                        to = S[0][:, at * P:(at + count) * P]
                    elif what == 0:
                        to = dst_T[:, at * P:(at + count) * P]
                    elif what == 1:
                        to = src_T[:, at * P:(at + count) * P]
                    else:
                        count_t = min(count * P, EDGE_TILES - at * P)
                        to, src = type_all[:, at * P:at * P + count_t], src[:, 0:count_t]
                    act.copy(to, src).then_inc(prep_kept, 1)

                def cursors(conv):
                    rows = row_all if conv < 2 else rel_row_all
                    weights = type_all if conv == 0 else weight_all
                    act.wait_ge(vec_prep, VEC_PREPARED)
                    with act.Fori(0, PAIRS) as i:
                        for half in range(2):
                            cols = ds(i * (2 * GROUP) + half * GROUP, GROUP)
                            act.wait_ge(cursor_free, GROUPS * conv + i * 2 + half + 1)
                            act.copy(row_cur[:, half, :], rows[:, cols]).then_inc(cursor_ready, 1)
                            act.copy(rel_cur[:, half, :], rel_all[:, cols]).then_inc(cursor_ready, 1)
                            if conv == 1:
                                act.copy(weight_cur[:, half, :], type_all[:, cols]).then_inc(cursor_ready, 1)
                            else:
                                act.copy(weight_cur[:, half, :], weights[:, cols]).then_inc(cursor_ready, 1)

                def deviations(which, c):
                    act.wait_ge(norm_step, c * 3 + (which * CHUNKS * 3 + 2))
                    act.activation(rstd[:, :], moments[:, :, 1], ACT.Sqrt, bias=eps[:, 0:1]).then_inc(deviation, 1)

                def norm_copies(c):
                    for b, (t, n) in enumerate(NORM_CUTS):
                        act.wait_ge(turned_back, c * 2 + b + 1)
                        act.copy(S[0][:, tile_cols(c, t, n)], bank[4 + b][:, 0:n * P]).then_inc(norm_kept, 1)
                        act.copy(chunk_in[:, 0, t * P:(t + n) * P], bank[4 + b][:, 0:n * P]).then_inc(chunk_kept[1], 1)
                    for u in range(2):
                        act.wait_ge(emb_psum, c * 2 + u + 1)
                        act.copy(S[1][:, node_cols(c, u)], bank[6 + u][:, 0:HALF]).then_inc(emb_kept, 1)
                        act.copy(chunk_in[:, 1, u * HALF:(u + 1) * HALF], bank[6 + u][:, 0:HALF]).then_inc(chunk_kept[1], 1)

                def keep_chunk(p, c):
                    act.wait_ge(updated[p], c * 2 + 2)
                    for h, src in enumerate(TABLE_IN[p]):
                        act.copy(chunk_in[:, h, :], src[:, node_cols2(c)]).then_inc(chunk_kept[p], 1)

                def table_copies(p, c):
                    copies = tile_copies(p)
                    n = 0
                    for t in range(TILES_PER_CHUNK):
                        act.wait_ge(row_stored[p][t % 2], c * (16 * slot_stores(t % 2)) + 16 * (t // 2))
                        for at, size in cuts(TABLE_COLS[p]):
                            act.wait_ge(table_psum[p], c * (TILES_PER_CHUNK * copies) + n + 1)
                            act.copy(stage[:, t % 2, at:at + size], bank[4 + n % 4][:, 0:size]).then_inc(table_copied[p], 1)
                            n += 1

                for conv in range(CONVS):
                    cursors(conv)
                    if conv < 4:
                        with act.Fori(0, CHUNKS) as c:
                            if conv < 2:
                                act.wait_ge(inverted, 3)
                                act.copy(chunk_in[:, 1, :], S[3][:, node_cols2(c)]).then_inc(counts_kept, 1)
                            if conv == 1:
                                deviations(0, c)
                                norm_copies(c)
                            else:
                                keep_chunk(conv, c)
                            table_copies(conv, c)
                    else:
                        with act.Fori(0, CHUNKS) as c:
                            deviations(1, c)

            @block.tensor
            def _(pe):
                pe.wait_ge(vec_prep, 7)
                pe.wait_ge(w_in, 16 * 14)
                for n, (what, at, count) in enumerate(FILLS):
                    if n == EDGE_FILLS:
                        pe.wait_ge(x_in, 16 * NODE_TILES)
                    if n >= 8:
                        pe.wait_ge(prep_kept, n - 7)
                    for m in range(count):
                        if what == "w":
                            block_in = w_raw[:, m, :]
                        elif what == "x":
                            block_in = x_tiles[:, at + m, :]
                        else:
                            block_in = edge_f[what][:, at + m, :]
                        mm = pe.transpose(bank[n % 8][:, m * P:(m + 1) * P], block_in, ident[:, :])
                    mm.then_inc(prep_psum, 1)
                pe.wait_ge(prep_kept, len(FILLS))

                pe.wait_ge(vec_prep, VEC_PREPARED)
                wide = pe.value_load(wide_i[0:1, 0:1], min_val=0, max_val=1)

                def group(conv, i, half):
                    g = i * 2 + half
                    seen = GROUPS * conv
                    if conv == 1:
                        base = pe.value_load(base_i[0:1, ds(g, 1)], min_val=0, max_val=N_NODES - 1)
                        pe.wait_ge(etype_hot_ready, g + 1)
                        pe.wait_ge(looked_up, g)
                        for k in range(GROUP):
                            mm = pe.matmul(bank[3 + k // 4][:, k % 4 * P:(k % 4 + 1) * P], etype_hot[:, k * P:(k + 1) * P],
                                           S[3][INVERSE, ds(base, P)], start=True, stop=True)
                            if k % 4 == 3 or k == GROUP - 1:
                                mm.then_inc(lookup_psum, 1)
                    pe.wait_ge(onehot_ready, g + (seen + 1))
                    for k in range(GROUP):
                        pe.wait_ge(gathered[half][k], i * 16 + 16 * (PAIRS * conv + 1))
                        for f in range(CONV_WIDTH[conv] // P):
                            mm = pe.matmul(bank[f][:, 0:P], message(conv, half, k, f), onehot[:, k, :],
                                           start=(k == 0), stop=(k == GROUP - 1))
                        if conv == 0:
                            mm = pe.matmul(bank[2][0:32, 0:P], typehot[:, k, :], onehot[:, k, :],
                                           start=(k == 0), stop=(k == GROUP - 1))
                    mm.then_inc(sums_psum, 1)
                    with pe.If(wide):
                        with pe.Fori(1, NODE_TILES) as j:
                            step = g * (NODE_TILES - 1) + j
                            pe.wait_ge(wide_onehot, step + seen * (NODE_TILES - 1))
                            if conv == 1:
                                for k in range(GROUP):
                                    mm = pe.matmul(bank[3 + k // 4][:, k % 4 * P:(k % 4 + 1) * P], etype_hot[:, k * P:(k + 1) * P],
                                                   S[3][INVERSE, ds(j * P, P)], start=True, stop=True)
                            for f in range(CONV_WIDTH[conv] // P):
                                for k in range(GROUP):
                                    mm = pe.matmul(bank[7][:, f * P:(f + 1) * P], message(conv, half, k, f), onehot[:, k, :],
                                                   start=(k == 0), stop=(k == GROUP - 1))
                            if conv == 0:
                                for k in range(GROUP):
                                    mm = pe.matmul(bank[7][0:32, 2 * P:3 * P], typehot[:, k, :], onehot[:, k, :],
                                                   start=(k == 0), stop=(k == GROUP - 1))
                            mm.then_inc(wide_psum, 1)

                def degrees(p, c):
                    for u in range(2):
                        pe.wait_ge(scaled, c * 2 + 2 * CHUNKS * p)
                        pe.wait_ge(counts_kept, c + (CHUNKS * p + 1))
                        pe.matmul(bank[6 + u][:, 0:HALF], ones[COUNT, :], chunk_in[COUNT, 1, u * HALF:(u + 1) * HALF],
                                  start=True, stop=True).then_inc(deg_psum, 1)

                def update(p, c):
                    for u in range(2):
                        pe.wait_ge(updated[p], c * 2)
                        if p == 0:
                            pe.wait_ge(scaled, c * 2 + u + 1)
                        for f, terms in enumerate(UPDATE[p]):
                            for n, (w, src) in enumerate(terms):
                                mm = pe.matmul(bank[u * len(UPDATE[p]) + f][:, 0:HALF], w, src[:, node_cols(c, u)],
                                               start=(n == 0), stop=(n == len(terms) - 1))
                        mm.then_inc(update_psum[p], 1)

                def turn(p, c):
                    pe.wait_ge(updated[p], c * 2 + 2)
                    for b, (t0, n) in enumerate(NORM_CUTS):
                        for t in range(n):
                            mm = pe.transpose(bank[2 + b][:, t * P:(t + 1) * P], chunk_in[:, 0, (t0 + t) * P:(t0 + t + 1) * P], ident[:, :])
                        mm.then_inc(turned, 1)

                def turn_back_and_embed(c):
                    pe.wait_ge(scaled, c * 2 + (2 * CHUNKS + 2))
                    for u in range(2):
                        pe.matmul(bank[6 + u][:, 0:HALF], emb[NTYPE, :], chunk_in[NTYPE, 1, u * HALF:(u + 1) * HALF],
                                  start=True, stop=True).then_inc(emb_psum, 1)
                    pe.wait_ge(normed_ready, c + 1)
                    for b, (t0, n) in enumerate(NORM_CUTS):
                        for t in range(n):
                            mm = pe.transpose(bank[4 + b][:, t * P:(t + 1) * P], normed[:, t0 + t, :], ident[:, :])
                        mm.then_inc(turned_back, 1)
                    pe.wait_ge(norm_kept, c * 2 + 2)
                    pe.wait_ge(emb_kept, c * 2 + 2)

                def table(p, c):
                    copies = tile_copies(p)
                    pe.wait_ge(chunk_kept[p], c * chunk_copies(p) + chunk_copies(p))
                    if p:
                        pe.wait_ge(table_w_in, 16 * [0, 2, 4, 5][p])
                    n = 0
                    for t in range(TILES_PER_CHUNK):
                        for at, size in cuts(TABLE_COLS[p]):
                            pe.wait_ge(table_copied[p], c * (TILES_PER_CHUNK * copies) + max(0, n - 3))
                            halves = TABLE_IN[p]
                            for h in range(len(halves)):
                                mm = pe.matmul(bank[4 + n % 4][:, 0:size], chunk_in[:, h, t * P:(t + 1) * P], table_weights(p, h, at, size),
                                               start=(h == 0), stop=(h == len(halves) - 1))
                            mm.then_inc(table_psum[p], 1)
                            n += 1

                for conv in range(CONVS):
                    with pe.Fori(0, PAIRS) as i:
                        for half in range(2):
                            group(conv, i, half)
                    pe.wait_ge(cursor_free, freed(conv))
                    with pe.Fori(0, CHUNKS) as c:
                        if conv < 2:
                            degrees(conv, c)
                        update(conv, c)
                        if conv in (1, 4):
                            turn(conv, c)
                        if conv == 1:
                            turn_back_and_embed(c)
                        if conv < 4:
                            table(conv, c)

            @block.vector
            def _(vec):
                def step(op, n):
                    op.then_inc(vec_prep, 1)
                    vec.wait_ge(vec_prep, n)

                vec.wait_ge(consts, 5)
                step(vec.tensor_copy(iota_f[:, :], iota_i[:, :]), 1)
                step(vec.tensor_copy(lane_f[:, :], lane_i[:, :]), 2)
                step(vec.tensor_scalar(ident[:, :], iota_f[:, :], lane_f[:, 0:1], None, ALU.is_equal), 3)
                vec.wait_ge(edges_in, 160)
                vec.wait_ge(types_padded, 32)
                for n in range(3):
                    step(vec.tensor_copy(edge_f[n], edge_i[n]), 4 + n)
                step(vec.tensor_scalar(S[3][NTYPE, 0:N_NODES], ntype_i, lane_f[NTYPE, 1:2], None, ALU.is_equal), 7)
                step(vec.tensor_reduce(tile_low[:, :], edge_f[0], AX.X, ALU.min), 8)
                step(vec.scalar_tensor_tensor(out=onehot[:, :, :], in0=edge_f[0], scalar=float(NO_NODE), in1=edge_f[0], op0=ALU.is_lt, op1=ALU.mult), 9)
                step(vec.tensor_reduce(tile_high[:, :], onehot[:, :, :], AX.X, ALU.max), 10)
                by_group = lambda v: v[:, 0:EDGE_TILES].rearrange("p (g k) -> p g k", k=GROUP)
                vec.wait_ge(bounds_in, 16)
                step(vec.tensor_reduce(base_f[:, :], by_group(bounds), AX.X, ALU.min), 11)
                vec.wait_ge(bounds_in, 32)
                step(vec.tensor_reduce(high_f[:, :], by_group(bounds), AX.X, ALU.max), 12)
                step(vec.tensor_tensor(span_f[:, :], high_f[:, :], base_f[:, :], ALU.subtract), 13)
                step(vec.tensor_reduce(wide_f[:, :], span_f[:, :], AX.X, ALU.max), 14)
                step(vec.tensor_scalar(wide_f[:, :], wide_f[:, :], float(P - 1), None, ALU.is_gt), 15)
                step(vec.tensor_scalar(narrow_f[:, :], wide_f[:, :], -1.0, 1.0, ALU.mult, ALU.add), 16)
                step(vec.tensor_scalar(base_f[:, :], base_f[:, :], narrow_f[:, 0:1], None, ALU.mult), 17)
                step(vec.tensor_copy(base_i[:, :], base_f[0:1, :]), 18)
                step(vec.tensor_copy(wide_i[:, :], wide_f[0:1, :]), 19)
                vec.wait_ge(prep_kept, EDGE_FILLS)
                step(vec.tensor_tensor(by_group(rel_all), by_group(dst_T), base_f[:, :].unsqueeze(2).broadcast_to([P, GROUPS, GROUP]), ALU.subtract), 20)
                step(vec.tensor_copy(row_all[:, :], src_T[:, 0:EDGE_TILES]), 21)
                step(vec.scalar_tensor_tensor(out=rel_row_all[:, :], in0=src_T[:, 0:EDGE_TILES], scalar=float(RELATIONS), in1=type_all[:, :], op0=ALU.mult, op1=ALU.add), VEC_PREPARED)
                vec.wait_ge(prep_kept, len(FILLS))
                vec.memset(S[1][:, :], 0.0).then_inc(zeroed, 1)
                vec.memset(S[2][:, :], 0.0).then_inc(zeroed, 1)
                vec.wait_ge(zeroed, 2)
                for n in range(2):
                    vec.sem_inc(cursor_free, 1)

                wide = vec.value_load(wide_i[0:1, 0:1], min_val=0, max_val=1)

                def build_onehots(conv, half, rel, signal):
                    for k in range(GROUP):
                        weight = dict(scalar2=weight_cur[:, half, k:k + 1], op1=ALU.mult) if conv >= 2 else dict(scalar2=None)
                        op = vec.tensor_scalar(onehot[:, k, :], iota_f[:, :], scalar1=rel(k), op0=ALU.is_equal, **weight)
                    op.then_inc(signal, 1)

                def add_sums(conv, source, window):
                    for f, sums in enumerate(SUMS[conv]):
                        op = vec.tensor_tensor(sums[:, window], sums[:, window], source[f], ALU.add)
                    if conv == 0:
                        op = vec.tensor_tensor(S[3][SUMMED, window], S[3][SUMMED, window], source[-1], ALU.add)
                    return op

                def group(conv, i, half):
                    g = i * 2 + half
                    seen = GROUPS * conv
                    base = vec.value_load(base_i[0:1, ds(g, 1)], min_val=0, max_val=N_NODES - 1)
                    vec.wait_ge(cursor_ready, g * CURSORS + CURSORS * (seen + 1))
                    if conv == 0:
                        vec.tensor_tensor(typehot[:, :, :], iota_f[:, 0:32].unsqueeze(1).broadcast_to([P, GROUP, 32]),
                                          weight_cur[:, half, :].unsqueeze(2).broadcast_to([P, GROUP, 32]), ALU.is_equal)
                    build_onehots(conv, half, lambda k: rel_cur[:, half, k:k + 1], onehot_ready)
                    if conv == 1:
                        vec.wait_ge(etype_in, g * 16 + 16)
                        vec.tensor_scalar(etype_hot, etype_row, lane_f[INVERSE, 0:1], None, ALU.is_equal).then_inc(etype_hot_ready, 1)
                        vec.wait_ge(onehot_ready, g + (seen + 1))
                        for k in range(GROUP):
                            if k % 4 == 0:
                                vec.wait_ge(lookup_psum, g * 4 + (k // 4 + 1))
                            op = vec.tensor_tensor_reduce(bank[3 + k // 4][:, k % 4 * P:(k % 4 + 1) * P], bank[3 + k // 4][:, k % 4 * P:(k % 4 + 1) * P], onehot[:, k, :], 1.0, 0.0,
                                                          ALU.mult, ALU.add, part[:, k:k + 1])
                        op.then_inc(looked_up, 1)
                    with vec.If(wide):
                        wide_windows(conv, g, half, seen)
                    if conv == 1:
                        vec.wait_ge(looked_up, g + 1)
                        vec.tensor_copy(weight_all[:, ds(g * GROUP, GROUP)], part[:, :])
                    vec.wait_ge(sums_psum, g + (seen + 1))
                    source = [bank[f][:, 0:P] for f in range(CONV_WIDTH[conv] // P)] + [bank[2][0:32, 0:P]]
                    add_sums(conv, source, ds(base, P)).then_inc(cursor_free, 1)
                    vec.wait_ge(cursor_free, g + (seen + 3))

                def wide_windows(conv, g, half, seen):
                    vec.wait_ge(sums_psum, g + (seen + 1))
                    if conv == 1:
                        vec.wait_ge(looked_up, g + 1)
                    rel_steps, part_steps = NODE_TILES, (NODE_TILES - 1)
                    vec.tensor_copy(rel_wide[:, :], rel_cur[:, half, :]).then_inc(wide_rel, 1)
                    with vec.Fori(1, NODE_TILES) as j:
                        done = g * (NODE_TILES - 1) + j + seen * (NODE_TILES - 1)
                        vec.wait_ge(wide_rel, g * rel_steps + j + seen * rel_steps)
                        vec.tensor_scalar(rel_wide[:, :], rel_wide[:, :], -float(P), None, ALU.add).then_inc(wide_rel, 1)
                        vec.wait_ge(wide_rel, g * rel_steps + j + (seen * rel_steps + 1))
                        build_onehots(conv, half, lambda k: rel_wide[:, k:k + 1], wide_onehot)
                        vec.wait_ge(wide_onehot, done)
                        vec.wait_ge(wide_psum, done)
                        if conv == 1:
                            for k in range(GROUP):
                                op = vec.tensor_tensor_reduce(bank[3 + k // 4][:, k % 4 * P:(k % 4 + 1) * P], bank[3 + k // 4][:, k % 4 * P:(k % 4 + 1) * P], onehot[:, k, :], 1.0, 0.0,
                                                              ALU.mult, ALU.add, part_wide[:, k:k + 1])
                            op.then_inc(wide_part, 1)
                            vec.wait_ge(wide_part, g * (2 * part_steps) + j * 2 - 1)
                            vec.tensor_tensor(part[:, :], part[:, :], part_wide[:, :], ALU.add).then_inc(wide_part, 1)
                            vec.wait_ge(wide_part, g * (2 * part_steps) + j * 2)
                        source = [bank[7][:, f * P:(f + 1) * P] for f in range(CONV_WIDTH[conv] // P)] + [bank[7][0:32, 2 * P:3 * P]]
                        add_sums(conv, source, ds(j * P, P))

                def scale_by_degree(p, c):
                    seen = 2 * CHUNKS * p
                    for u in range(2):
                        vec.wait_ge(deg_psum, c * 2 + (seen + u + 1))
                        vec.tensor_scalar(inv_deg[:, u, :], bank[6 + u][:, 0:HALF], 1.0, None, ALU.max).then_inc(deg_step, 1)
                        vec.wait_ge(deg_step, c * 4 + (2 * seen + 2 * u + 1))
                        vec.reciprocal(inv_deg[:, u, :], inv_deg[:, u, :]).then_inc(deg_step, 1)
                        vec.wait_ge(deg_step, c * 4 + (2 * seen + 2 * u + 2))
                        sums = S[1 + p][:, node_cols(c, u)]
                        vec.tensor_tensor(sums, sums, inv_deg[:, u, :], ALU.mult).then_inc(scaled, 1)

                def invert_counts():
                    vec.tensor_copy(S[3][COUNT, :], S[3][SUMMED, :]).then_inc(inverted, 1)
                    vec.wait_ge(inverted, 1)
                    vec.tensor_scalar(S[3][INVERSE, :], S[3][INVERSE, :], 1.0, None, ALU.max).then_inc(inverted, 1)
                    vec.wait_ge(inverted, 2)
                    vec.reciprocal(S[3][INVERSE, :], S[3][INVERSE, :]).then_inc(inverted, 1)
                    vec.wait_ge(inverted, 3)

                def update(p, c):
                    for u in range(2):
                        cols = node_cols(c, u)
                        vec.wait_ge(update_psum[p], c * 2 + u + 1)
                        if p == 0:
                            vec.tensor_scalar(S[1][:, cols], bank[u][:, 0:HALF], BIAS[0][0], 0.0, ALU.add, ALU.max).then_inc(updated[p], 1)
                            continue
                        if p == 1:
                            vec.wait_ge(scaled, 2 * CHUNKS + c * 2 + u + 1)
                        for f, sums in enumerate(SUMS[p]):
                            op = vec.scalar_tensor_tensor(out=sums[:, cols], in0=bank[u * len(SUMS[p]) + f][:, 0:HALF], scalar=BIAS[p][f],
                                                          in1=sums[:, cols], op0=ALU.add, op1=ALU.add)
                        op.then_inc(update_step[p], 1)
                        vec.wait_ge(update_step[p], c * 2 + u + 1)
                        if p == 1:
                            vec.wait_ge(table_psum[1], c * (TILES_PER_CHUNK * tile_copies(1)))
                        for f, sums in enumerate(SUMS[p]):
                            fixed = chunk_in[:, 0, u * HALF:(u + 1) * HALF]
                            if p == 1:
                                op = vec.tensor_tensor(fixed, sums[:, cols], S[0][:, cols], ALU.add)
                            elif p == 4:
                                op = vec.scalar_tensor_tensor(out=fixed, in0=sums[:, cols], scalar=0.0, in1=S[0][:, cols], op0=ALU.max, op1=ALU.add)
                            else:
                                op = vec.tensor_scalar(sums[:, cols], sums[:, cols], 0.0, None, ALU.max)
                        op.then_inc(updated[p], 1)

                def norm(which, c):
                    seen = CHUNKS * which
                    steps = 3
                    for b, (t0, n) in enumerate(NORM_CUTS):
                        vec.wait_ge(turned, c * 2 + (2 * seen + b + 1))
                        for t in range(n):
                            op = vec.bn_stats(stats[:, t0 + t, :], bank[2 + b][:, t * P:(t + 1) * P])
                    op.then_inc(norm_step, 1)
                    vec.wait_ge(norm_step, c * steps + (seen * steps + 1))
                    vec.sem_inc(moments_begun, 1)
                    for t in range(TILES_PER_CHUNK):
                        op = vec.bn_aggr(moments[:, t, :], stats[:, t, :])
                    op.then_inc(norm_step, 1)
                    vec.wait_ge(norm_step, c * steps + (seen * steps + 2))
                    vec.wait_ge(deviation, c + (seen + 1))
                    vec.reciprocal(rstd[:, :], rstd[:, :]).then_inc(norm_step, 1)
                    vec.wait_ge(norm_step, c * steps + (seen * steps + 3))
                    if which == 0:
                        vec.wait_ge(turned_back, c * 2)
                    else:
                        vec.wait_ge(out_stored, c * 16)
                    for b, (t0, n) in enumerate(NORM_CUTS):
                        for t in range(n):
                            op = vec.tensor_scalar(normed[:, t0 + t, :], bank[2 + b][:, t * P:(t + 1) * P],
                                                   moments[:, t0 + t, 0:1], rstd[:, t0 + t:t0 + t + 1], ALU.subtract, ALU.mult)
                    op.then_inc(normed_ready, 1)

                def zero(p, arrays):
                    vec.wait_ge(table_psum[p], CHUNKS * TILES_PER_CHUNK * tile_copies(p))
                    for s in arrays:
                        op = vec.memset(s[:, :], 0.0)
                    op.then_inc(zeroed, 1)
                    vec.wait_ge(zeroed, 2 + p)

                for conv in range(CONVS):
                    with vec.Fori(0, PAIRS) as i:
                        for half in range(2):
                            group(conv, i, half)
                    if conv == 0:
                        invert_counts()
                    with vec.Fori(0, CHUNKS) as c:
                        if conv < 2:
                            scale_by_degree(conv, c)
                        update(conv, c)
                        if conv in (1, 4):
                            norm(conv // 4, c)
                    if 1 <= conv <= 3:
                        zero(conv, [None, [S[2], S[3]], [S[1]], [S[2]]][conv])


_INS = ['x', 'src', 'dst', 'edge_type_5', 'node_type_3', 'L0_gnn_W1l', 'L0_gnn_b1l', 'L0_gnn_W1r', 'L0_gnn_W2l', 'L0_gnn_b2l',
        'L0_gnn_W2r', 'L1_gnn_node_emb', 'L1_gnn_W1', 'L1_gnn_root1', 'L1_gnn_b1', 'L1_gnn_W2', 'L1_gnn_root2', 'L1_gnn_b2',
        'L1_gnn_W3', 'L1_gnn_root3', 'L1_gnn_b3']


def kernel(**inputs):
    import numpy as np
    import concourse.bacc as bacc
    from concourse import mybir as mb
    from concourse.bass_utils import run_bass_kernel_spmd as run

    nc = bacc.Bacc("TRN2", target_bir_lowering=False, num_devices=1)
    arrays, aps = {}, {}
    for name in _INS:
        v = np.ascontiguousarray(inputs[name])
        arrays[f"in_{name}"] = v
        aps[name] = nc.dram_tensor(f"in_{name}", v.shape, mb.dt.from_np(v.dtype), kind="ExternalInput").ap()
    out = nc.dram_tensor("out", (N_NODES, FEAT), mb.dt.float32, kind="ExternalOutput").ap()
    resnorm_gnn(nc, aps, out)
    return run(nc, [arrays], core_ids=[0]).results[0]["out"]
```

```python
from contextlib import ExitStack

import concourse.bass as bass
from concourse import mybir

P = 128
N_NODES = 6250
N_EDGES = 206250
FEAT = 128
WIDE = 256
RELATIONS = 5
NODE_TYPES = 3
EPS = 1e-5

NODE_TILES = -(-N_NODES // P)
NODES_PADDED = NODE_TILES * P
CHUNK_TILES = 4
CHUNK = CHUNK_TILES * P
FULL_CHUNKS = NODE_TILES // CHUNK_TILES
LAST_TILES = NODE_TILES - FULL_CHUNKS * CHUNK_TILES
assert LAST_TILES == 1
ACC_COLS = NODES_PADDED + P

EDGE_TILES = -(-N_EDGES // P)
GROUP = 13
GROUPS = EDGE_TILES // GROUP
assert GROUPS * GROUP == EDGE_TILES and GROUPS % 2 == 0
PAIRS = GROUPS // 2
SLOTS = 10
STRETCHES = 12
CHUNK_SLOT = 4
STRETCH_PAIRS = SLOTS // 2
assert STRETCHES * SLOTS <= GROUPS and (STRETCHES - 1) == FULL_CHUNKS - 1
EDGE_BLOCKS = -(-EDGE_TILES // P)
FULL_BLOCKS = EDGE_TILES // P
LAST_ROWS = N_EDGES // P - FULL_BLOCKS * P
LAST_NODES = N_NODES - (NODE_TILES - 1) * P
LAST_EDGES = N_EDGES % P
NO_NODE = 1000000

CONV_WIDTH = [FEAT, FEAT, WIDE, FEAT, FEAT]
CONVS = len(CONV_WIDTH)


def resnorm_gnn(nc, a, out):
    f32, i32 = mybir.dt.float32, mybir.dt.int32
    ALU, ACT, AX = mybir.AluOpType, mybir.ActivationFunctionType, mybir.AxisListType
    ds = bass.ds

    table_h = nc.dram_tensor("table_h", (NODES_PADDED, FEAT), f32).ap()
    table_1 = nc.dram_tensor("table_1", (NODES_PADDED, RELATIONS * WIDE), f32).ap()
    table_2 = nc.dram_tensor("table_2", (NODES_PADDED, RELATIONS * FEAT), f32).ap()
    table_3 = nc.dram_tensor("table_3", (NODES_PADDED, RELATIONS * FEAT), f32).ap()
    per_relation = lambda t: t.rearrange("n (r f) -> (n r) f", r=RELATIONS)
    GATHERED = [a["x"], table_h, per_relation(table_1), per_relation(table_2), per_relation(table_3)]
    STORED = [table_h, table_1, table_2, table_3]
    bounds_d = nc.dram_tensor("bounds_d", (2, EDGE_BLOCKS * P), f32).ap()
    types_d = nc.dram_tensor("types_d", (1, EDGE_TILES * P), i32).ap()

    ctx = ExitStack()
    with ctx:
        sb = lambda name, shape, dt=f32: ctx.enter_context(nc.sbuf_tensor(name, shape, dt))
        sem = lambda name: ctx.enter_context(nc.semaphore(name))

        S = [sb(f"S{n}", [P, ACC_COLS]) for n in range(4)]
        SUMMED, INVERSE, COUNT, NTYPE = slice(0, 32), slice(0, RELATIONS), slice(32, 64), slice(64, 64 + NODE_TYPES)
        msgs = sb("msgs", [P, 2 * GROUP * WIDE])
        onehot = sb("onehot", [P, 2, GROUP, P])
        row_all = sb("row_all", [P, EDGE_TILES], i32)
        rel_all = sb("rel_all", [P, EDGE_TILES])
        type_all = sb("type_all", [P, EDGE_TILES])
        weight_all = type_all
        row_cur = sb("row_cur", [P, 2, GROUP], i32)
        rel_cur = sb("rel_cur", [P, 2, GROUP])
        weight_cur = sb("weight_cur", [P, 2, GROUP])
        rel_wide = sb("rel_wide", [P, GROUP])
        typehot = sb("typehot", [P, 2, GROUP, 32])
        part = sb("part", [P, 2, GROUP])
        part_wide = sb("part_wide", [P, GROUP])
        base_f = sb("base_f", [P, GROUPS])
        wide_f = sb("wide_f", [P, 1])
        narrow_f = sb("narrow_f", [P, 1])
        base_i = sb("base_i", [1, GROUPS], i32)
        wide_i = sb("wide_i", [1, 1], i32)
        tile_low = sb("tile_low", [P, EDGE_BLOCKS])
        tile_high = sb("tile_high", [P, EDGE_BLOCKS])
        iota_f = sb("iota_f", [P, P])
        lane_i = sb("lane_i", [P, 2], i32)
        lane_f = sb("lane_f", [P, 2])
        ident = sb("ident", [P, P])
        ones = sb("ones", [P, P])
        eps = sb("eps", [P, 1])
        zeros = sb("zeros", [P, 1])
        bias = sb("bias", [P, 6])
        w_T = sb("w_T", [P, 4, P])
        emb = sb("emb", [P, FEAT])
        table_w = sb("table_w", [P, 2 * RELATIONS * WIDE])
        root1 = sb("root1", [P, 2, WIDE])
        root2 = sb("root2", [P, 2, FEAT])
        root3 = sb("root3", [P, FEAT])
        chunk_in = sb("chunk_in", [P, 2, CHUNK])
        inv_deg = sb("inv_deg", [P, CHUNK])
        stats = sb("stats", [P, CHUNK_TILES, 6])
        moments = sb("moments", [P, CHUNK_TILES, 2])
        rstd = sb("rstd", [P, CHUNK_TILES])
        normed = sb("normed", [P, CHUNK_TILES, P])
        stage = sb("stage", [P, 2, RELATIONS * WIDE])
        early = stage[:, :, :].rearrange("p s f -> p (s f)")
        limit_i = early[:, 0:STRETCHES * SLOTS].bitcast(i32)
        limit_f = early[:, P:P + STRETCHES * SLOTS]
        high_f = early[:, 2 * P:2 * P + GROUPS]
        span_f = early[:, 3 * P:3 * P + GROUPS]
        iota_i = early[:, 4 * P:5 * P].bitcast(i32)
        ordered_f = sb("ordered_f", [P, 1])
        ordered_i = sb("ordered_i", [1, 1], i32)
        etype_row_t = sb("etype_row", [P, GROUP * P], i32)

        bank = [ctx.enter_context(nc.psum_tensor(f"bank{n}", [P, 512], f32)) for n in range(8)]

        x_tiles = msgs[:, 0:NODE_TILES * P].rearrange("p (t f) -> p t f", f=P)
        edge_cols = EDGE_BLOCKS * P
        edge_f = [S[2][:, n * edge_cols:(n + 1) * edge_cols].rearrange("p (b c) -> p b c", c=P) for n in range(3)]
        edge_i = [v.bitcast(i32) for v in edge_f]
        src_T = S[1][:, 0:edge_cols]
        dst_T = S[1][:, edge_cols:2 * edge_cols]
        ntype_i = S[3][NTYPE, 0:N_NODES].bitcast(i32)
        etype_row = etype_row_t[INVERSE, :]
        w_raw = etype_row_t[:, 0:4 * P].bitcast(f32).rearrange("p (n f) -> p n f", n=4)
        etype_hot = msgs[INVERSE, 2 * GROUP * FEAT:2 * GROUP * (FEAT + P)].rearrange("p (h c) -> p h c", h=2)
        bounds = onehot[:, 0, :, :].rearrange("p k c -> p (k c)")

        def message(conv, half, k, f):
            w = CONV_WIDTH[conv]
            at = (half * GROUP + k) * w
            return msgs[:, at + f * P:at + (f + 1) * P]

        def message_row(conv, half, k):
            w = CONV_WIDTH[conv]
            at = (half * GROUP + k) * w
            return msgs[:, at:at + w]

        SUMS = [[S[1]], [S[2]], [S[2], S[3]], [S[1]], [S[2]]]

        UPDATE = [
            [[(w_T[:, 0, :], S[1]), (w_T[:, 1, :], S[0])]],
            [[(w_T[:, 3, :], S[1])]],
            [[(root1[:, 0, f * P:(f + 1) * P], S[0]), (root1[:, 1, f * P:(f + 1) * P], S[1])] for f in range(2)],
            [[(root2[:, 0, :], S[2]), (root2[:, 1, :], S[3])]],
            [[(root3[:, :], S[1])]],
        ]
        BIAS = [[bias[:, 0:1]], [bias[:, 1:2]], [bias[:, 2:3], bias[:, 3:4]], [bias[:, 4:5]], [bias[:, 5:6]]]
        TABLE_IN = [[S[1]], [S[0], S[1]], [S[2], S[3]], [S[1]]]
        TABLE_COLS = [FEAT, RELATIONS * WIDE, RELATIONS * FEAT, RELATIONS * FEAT]

        def table_weights(p, h, at, n):
            return w_T[:, 2, :] if p == 0 else table_w[:, h * TABLE_COLS[p] + at:h * TABLE_COLS[p] + at + n]

        cuts = lambda n: [(c, min(512, n - c)) for c in range(0, n, 512)]
        chunk_cols = lambda c, tiles: ds(c * CHUNK, tiles * P)
        tile_rows = lambda c, t: ds(c * CHUNK + t * P, P)
        chunk_copies = lambda p: 2 if p == 1 else len(TABLE_IN[p])
        TILE_SLOTS = [{1: [0], 2: [1], 3: [2], 4: [3]}] * 4
        TILE_SLOTS[1] = {2: [0], 3: [1, 2], 4: [3]}
        COUNT_BANK, LOOKUP_BANKS, WIDE_BANK = 2, (3, 4), 7
        DEGREE_BANK, EMB_BANK, BACK_BANK = 7, 6, 5
        UPDATE_BANKS = [(1,), (1,), (2, 3), (2,), (2,)]
        TURN_BANK = [None, 2, None, None, 3]
        TABLE_BANKS = (5, 6)
        LOOKUP_FILLS = -(-GROUP // 4)

        padded, edges_in, types_padded, x_in, w_in = sem("padded"), sem("edges_in"), sem("types_padded"), sem("x_in"), sem("w_in")
        bounds_out, bounds_in = sem("bounds_out"), sem("bounds_in")
        table_w_in = sem("table_w_in")
        consts = sem("consts")
        vec_prep = sem("vec_prep")
        prep_psum, prep_kept = sem("prep_psum"), sem("prep_kept")
        inverting = sem("inverting")
        inverted = sem("inverted")
        zeroed = sem("zeroed")
        rel_rows_made, zeroing = sem("rel_rows_made"), sem("zeroing")
        branches_joined = sem("branches_joined")
        cursor_free, cursor_ready = sem("cursor_free"), sem("cursor_ready")
        lookups_begun = sem("lookups_begun")
        gathers_begun, moments_begun = sem("gathers_begun"), sem("moments_begun")
        gathered = [[sem(f"gathered{h}_{k}") for k in range(GROUP)] for h in range(2)]
        onehot_ready, sums_psum = sem("onehot_ready"), sem("sums_psum")
        etype_in, etype_hot_ready = sem("etype_in"), sem("etype_hot_ready")
        lookup_psum, looked_up, weighed = sem("lookup_psum"), sem("looked_up"), sem("weighed")
        wide_lookup, wide_looked_up = sem("wide_lookup"), sem("wide_looked_up")
        wide_onehot, wide_psum, wide_rel, wide_part = sem("wide_onehot"), sem("wide_psum"), sem("wide_rel"), sem("wide_part")
        deg_psum, deg_step, scaled = sem("deg_psum"), sem("deg_step"), sem("scaled")
        update_psum = [sem(f"update_psum{p}") for p in range(CONVS)]
        update_step = [sem(f"update_step{p}") for p in range(CONVS)]
        updated = [sem(f"updated{p}") for p in range(CONVS)]
        counts_kept = sem("counts_kept")
        chunk_kept = [sem(f"chunk_kept{p}") for p in range(4)]
        turned, deviation, norm_step, normed_ready = sem("turned"), sem("deviation"), sem("norm_step"), sem("normed_ready")
        turned_back, norm_kept = sem("turned_back"), sem("norm_kept")
        emb_psum, emb_kept = sem("emb_psum"), sem("emb_kept")
        table_psum = [sem(f"table_psum{p}") for p in range(4)]
        table_copied = [sem(f"table_copied{p}") for p in range(4)]
        row_stored = [[sem(f"row_stored{p}_{s}") for s in range(2)] for p in range(4)]
        out_stored = sem("out_stored")

        CURSORS = 3
        freed = lambda conv: 2 + GROUPS * (conv + 1)
        stores_in_all = lambda place: FULL_CHUNKS * 2 + (1 if place == 0 else 0)
        tile_copies = lambda p: len(cuts(TABLE_COLS[p]))
        VEC_PREPARED = 28
        FILLS = [("w", 0, 4)]
        FILLS += [(n, b, min(4, EDGE_BLOCKS - b)) for n in range(3) for b in range(0, EDGE_BLOCKS, 4)]
        EDGE_FILLS = len(FILLS)
        FILLS += [("x", t, min(4, NODE_TILES - t)) for t in range(0, NODE_TILES, 4)]

        with nc.Block() as block:

            @block.sync
            def _(sp):
                sp.wait_ge(padded, 5)
                full = FULL_BLOCKS * P * P
                whole = full + LAST_ROWS * P
                for n, name in enumerate(["dst", "src", "edge_type_5"]):
                    e = a[name]
                    sp.dma_start(edge_i[n][:, 0:FULL_BLOCKS, :], e[0:full].rearrange("(b r c) -> r b c", r=P, c=P)).then_inc(edges_in, 16)
                    sp.dma_start(edge_i[n][0:LAST_ROWS, FULL_BLOCKS, :], e[full:whole].rearrange("(r c) -> r c", c=P)).then_inc(edges_in, 16)
                    sp.dma_start(edge_i[n][LAST_ROWS:LAST_ROWS + 1, FULL_BLOCKS, 0:LAST_EDGES], e[whole:N_EDGES].rearrange("(o c) -> o c", o=1)).then_inc(edges_in, 16)
                sp.dma_start(ntype_i, a["node_type_3"].rearrange("(o n) -> o n", o=1).broadcast_to([NODE_TYPES, N_NODES])).then_inc(edges_in, 16)
                for n, name in enumerate(["L0_gnn_W1l", "L0_gnn_W1r", "L0_gnn_W2l", "L0_gnn_W2r"]):
                    sp.dma_start(w_raw[:, n, :], a[name]).then_inc(w_in, 16)
                with sp.Fori(0, NODE_TILES - 1) as t:
                    sp.dma_start(msgs[:, ds(t * P, P)], a["x"][ds(t * P, P), :]).then_inc(x_in, 16)
                sp.dma_start(x_tiles[0:LAST_NODES, NODE_TILES - 1, :], a["x"][(NODE_TILES - 1) * P:N_NODES, :]).then_inc(x_in, 16)
                for n, name in enumerate(["L0_gnn_b1l", "L0_gnn_b2l"]):
                    sp.dma_start(bias[:, n:n + 1], a[name].rearrange("(p o) -> p o", o=1)).then_inc(w_in, 16)
                for f in range(2):
                    sp.dma_start(bias[:, 2 + f:3 + f], a["L1_gnn_b1"][f * P:(f + 1) * P].rearrange("(p o) -> p o", o=1)).then_inc(w_in, 16)
                for n, name in enumerate(["L1_gnn_b2", "L1_gnn_b3"]):
                    sp.dma_start(bias[:, 4 + n:5 + n], a[name].rearrange("(p o) -> p o", o=1)).then_inc(w_in, 16)
                sp.dma_start(emb[NTYPE, :], a["L1_gnn_node_emb"]).then_inc(w_in, 16)
                sp.dma_start(root1[:, :, :], a["L1_gnn_root1"].rearrange("(h p) o -> p h o", p=P)).then_inc(w_in, 16)
                sp.dma_start(root2[:, :, :], a["L1_gnn_root2"].rearrange("(h p) o -> p h o", p=P)).then_inc(w_in, 16)
                sp.dma_start(root3[:, :], a["L1_gnn_root3"]).then_inc(w_in, 16)

                def load_table_weights(p, name):
                    n = TABLE_COLS[p]
                    for h in range(len(TABLE_IN[p])):
                        sp.dma_start(table_w[:, h * n:(h + 1) * n].rearrange("p (r o) -> p r o", r=RELATIONS),
                                     a[name][:, h * P:(h + 1) * P, :].rearrange("r p o -> p r o")).then_inc(table_w_in, 16)

                load_table_weights(1, "L1_gnn_W1")
                sp.dma_start(types_d[0, 0:N_EDGES].rearrange("(r c) -> r c", c=1650), a["edge_type_5"].rearrange("(r c) -> r c", c=1650)).then_inc(types_padded, 16)
                sp.wait_ge(edges_in, 160)
                sp.dma_start(types_d[0:1, N_EDGES:EDGE_TILES * P], edge_i[2][LAST_ROWS:LAST_ROWS + 1, FULL_BLOCKS, LAST_EDGES:P]).then_inc(types_padded, 16)
                sp.wait_ge(vec_prep, 10)
                for n, t in enumerate([tile_low, tile_high]):
                    sp.dma_start(bounds_d[n, :].rearrange("(b r) -> r b", r=P), t[:, :], allow_slow_non_contiguous=True).then_inc(bounds_out, 16)
                sp.wait_ge(bounds_out, 32)
                sp.dma_start(bounds, bounds_d[0:1, :].broadcast_to([P, edge_cols])).then_inc(bounds_in, 16)
                sp.wait_ge(vec_prep, 11)
                sp.dma_start(bounds, bounds_d[1:2, :].broadcast_to([P, edge_cols])).then_inc(bounds_in, 16)

                sp.wait_ge(types_padded, 32)
                sp.wait_ge(prep_kept, len(FILLS))
                with sp.Fori(0, GROUPS) as g:
                    sp.wait_ge(etype_hot_ready, g)
                    sp.dma_start(etype_row, types_d[0:1, ds(g * (GROUP * P), GROUP * P)].broadcast_to([RELATIONS, GROUP * P])).then_inc(etype_in, 16)
                sp.wait_ge(table_psum[1], NODE_TILES * tile_copies(1))
                load_table_weights(2, "L1_gnn_W2")
                sp.wait_ge(table_psum[2], NODE_TILES * tile_copies(2))
                load_table_weights(3, "L1_gnn_W3")

                with sp.Fori(0, FULL_CHUNKS) as c:
                    sp.wait_ge(normed_ready, c + (FULL_CHUNKS + 2))
                    sp.dma_start(out[ds(c * CHUNK, CHUNK), :].rearrange("(t p) f -> p t f", p=P), normed[:, :, :]).then_inc(out_stored, 16)
                sp.wait_ge(normed_ready, 2 * (FULL_CHUNKS + 1))
                sp.dma_start(out[FULL_CHUNKS * CHUNK:N_NODES, :], normed[0:LAST_NODES, 0, :]).then_inc(out_stored, 16)
                sp.wait_ge(out_stored, 16 * (FULL_CHUNKS + 1))

            @block.gpsimd
            def _(pool):
                pool.memset(edge_i[0][:, FULL_BLOCKS, :], NO_NODE).then_inc(padded, 1)
                pool.memset(edge_i[1][:, FULL_BLOCKS, :], 0).then_inc(padded, 1)
                pool.memset(edge_i[2][:, FULL_BLOCKS, :], 0).then_inc(padded, 1)
                pool.memset(x_tiles[:, NODE_TILES - 1, :], 0.0).then_inc(padded, 1)
                pool.memset(S[3][:, :], 0.0).then_inc(padded, 1)
                pool.iota(iota_i[:, :], [[1, P]], base=0, channel_multiplier=0).then_inc(consts, 1)
                pool.iota(limit_i[:, :], [[CHUNK, STRETCHES], [0, SLOTS]], base=0, channel_multiplier=0).then_inc(consts, 1)
                for n, start in enumerate([0, NTYPE.start]):
                    pool.iota(lane_i[:, n:n + 1], [[0, 1]], base=-start, channel_multiplier=1).then_inc(consts, 1)
                pool.memset(ones[:, :], 1.0).then_inc(consts, 1)
                pool.memset(eps[:, :], EPS).then_inc(consts, 1)
                pool.memset(zeros[:, :], 0.0).then_inc(consts, 1)
                pool.wait_ge(prep_kept, len(FILLS))

                for conv in range(CONVS):
                    width = CONV_WIDTH[conv]
                    if conv:
                        for s in range(2):
                            pool.wait_ge(row_stored[conv - 1][s], 16 * stores_in_all(s))
                    with pool.Fori(0, PAIRS) as i:
                        for half in range(2):
                            pool.wait_ge(cursor_ready, CURSORS * GROUPS * conv + i * (2 * CURSORS) + CURSORS * (half + 1))
                            pool.sem_inc(gathers_begun, 1)
                            for k in range(GROUP):
                                at = (half * GROUP + k) * width
                                pool.indirect_dma_start(
                                    msgs[:, at:at + width], None, GATHERED[conv],
                                    bass.IndirectOffsetOnAxis(ap=row_cur[:, half, k:k + 1], axis=0),
                                ).then_inc(gathered[half][k], 16)

            @block.scalar
            def _(act):
                for n, (what, at, count) in enumerate(FILLS):
                    if n == EDGE_FILLS:
                        act.wait_ge(padded, 5)
                    act.wait_ge(prep_psum, n + 1)
                    src = bank[n % 8][:, 0:count * P]
                    if what == "w":
                        to = w_T[:, :, :].rearrange("p n f -> p (n f)")
                    elif what == "x":
                        to = S[0][:, at * P:(at + count) * P]
                    elif what == 0:
                        to = dst_T[:, at * P:(at + count) * P]
                    elif what == 1:
                        to = src_T[:, at * P:(at + count) * P]
                    else:
                        count_t = min(count * P, EDGE_TILES - at * P)
                        to, src = type_all[:, at * P:at * P + count_t], src[:, 0:count_t]
                    act.copy(to, src).then_inc(prep_kept, 1)

                act.wait_ge(vec_prep, VEC_PREPARED)
                ordered = act.value_load(ordered_i[0:1, 0:1], min_val=0, max_val=1)

                def group(conv, i, half):
                    cols = ds(i * (2 * GROUP) + half * GROUP, GROUP)
                    act.wait_ge(cursor_free, i * 2 + (GROUPS * conv + half + 1))
                    act.copy(row_cur[:, half, :], row_all[:, cols]).then_inc(cursor_ready, 1)
                    if conv == 1:
                        act.copy(rel_cur[:, half, :], rel_all[:, cols]).then_inc(cursor_ready, 2)
                    else:
                        act.copy(rel_cur[:, half, :], rel_all[:, cols]).then_inc(cursor_ready, 1)
                        act.copy(weight_cur[:, half, :], type_all[:, cols]).then_inc(cursor_ready, 1)

                def table_rows(p, c, t):
                    copies = tile_copies(p)
                    act.wait_ge(row_stored[p][t % 2], c * 32 + 16 * (t // 2))
                    for n, (at, size) in enumerate(cuts(TABLE_COLS[p])):
                        act.wait_ge(table_psum[p], c * (CHUNK_TILES * copies) + (t * copies + n + 1))
                        act.copy(stage[:, t % 2, at:at + size], bank[TABLE_BANKS[(t * copies + n) % 2]][:, 0:size]).then_inc(table_copied[p], 1)
                    act.wait_ge(table_copied[p], c * (CHUNK_TILES * copies) + (t + 1) * copies)
                    act.dma_start(STORED[p][tile_rows(c, t), :], stage[:, t % 2, 0:TABLE_COLS[p]]).then_inc(row_stored[p][t % 2], 16)

                def chunk_slice(conv, c, slot, tiles):
                    at = slot - CHUNK_SLOT
                    cols = chunk_cols(c, tiles)
                    if at == 0 and conv < 2:
                        act.wait_ge(inverted, c * 3 + 3)
                        act.copy(chunk_in[:, 1, 0:tiles * P], S[3][:, cols]).then_inc(counts_kept, 1)
                    if at == 1 and conv in (0, 2, 3):
                        act.wait_ge(updated[conv], c + 1)
                        for h, src in enumerate(TABLE_IN[conv]):
                            act.copy(chunk_in[:, h, 0:tiles * P], src[:, cols]).then_inc(chunk_kept[conv], 1)
                    if at == 2 and conv in (1, 4):
                        seen = (FULL_CHUNKS + 1) * (conv // 4)
                        act.wait_ge(norm_step, c * 3 + (seen * 3 + 2))
                        act.activation(rstd[:, 0:tiles], moments[:, 0:tiles, 1], ACT.Sqrt, bias=eps[:, 0:1]).then_inc(deviation, 1)
                    if at == 3 and conv == 1:
                        act.wait_ge(emb_psum, c + 1)
                        act.copy(S[1][:, cols], bank[EMB_BANK][:, 0:tiles * P]).then_inc(emb_kept, 1)
                        act.copy(chunk_in[:, 1, 0:tiles * P], bank[EMB_BANK][:, 0:tiles * P]).then_inc(chunk_kept[1], 1)
                        act.wait_ge(turned_back, c + 1)
                        act.copy(S[0][:, cols], bank[BACK_BANK][:, 0:tiles * P]).then_inc(norm_kept, 1)
                        act.copy(chunk_in[:, 0, 0:tiles * P], bank[BACK_BANK][:, 0:tiles * P]).then_inc(chunk_kept[1], 1)
                    if conv < 4:
                        for t in TILE_SLOTS[conv].get(at - 1, []):
                            if t < tiles:
                                table_rows(conv, c, t)

                for conv in range(CONVS):
                    group(conv, 0, 0)
                    with act.If(ordered):
                        with act.Fori(0, STRETCH_PAIRS) as i:
                            for half in range(2):
                                group(conv, i + half, 1 - half)
                        with act.Fori(1, STRETCHES) as o:
                            for slot in range(SLOTS):
                                group(conv, o * STRETCH_PAIRS + (slot + 1) // 2, (slot + 1) % 2)
                                chunk_slice(conv, o - 1, slot, CHUNK_TILES)
                    with act.Else():
                        with act.Fori(0, STRETCHES * STRETCH_PAIRS) as i:
                            for half in range(2):
                                group(conv, i + half, 1 - half)
                    for g in range(STRETCHES * SLOTS + 1, GROUPS):
                        group(conv, g // 2, g % 2)
                    with act.If(ordered):
                        act.sem_inc(branches_joined, 1)
                    with act.Else():
                        with act.Fori(0, FULL_CHUNKS - 1) as c:
                            for slot in range(CHUNK_SLOT, SLOTS):
                                chunk_slice(conv, c, slot, CHUNK_TILES)
                    for c, tiles in ((FULL_CHUNKS - 1, CHUNK_TILES), (FULL_CHUNKS, LAST_TILES)):
                        for slot in range(CHUNK_SLOT, SLOTS):
                            chunk_slice(conv, c, slot, tiles)

            @block.tensor
            def _(pe):
                pe.wait_ge(vec_prep, 7)
                pe.wait_ge(w_in, 16 * 14)
                for n, (what, at, count) in enumerate(FILLS):
                    if n == EDGE_FILLS:
                        pe.wait_ge(x_in, 16 * NODE_TILES)
                    if n >= 8:
                        pe.wait_ge(prep_kept, n - 7)
                    for m in range(count):
                        if what == "w":
                            block_in = w_raw[:, m, :]
                        elif what == "x":
                            block_in = x_tiles[:, at + m, :]
                        else:
                            block_in = edge_f[what][:, at + m, :]
                        mm = pe.transpose(bank[n % 8][:, m * P:(m + 1) * P], block_in, ident[:, :])
                    mm.then_inc(prep_psum, 1)
                pe.wait_ge(prep_kept, len(FILLS))

                pe.wait_ge(vec_prep, VEC_PREPARED)
                wide = pe.value_load(wide_i[0:1, 0:1], min_val=0, max_val=1)
                ordered = pe.value_load(ordered_i[0:1, 0:1], min_val=0, max_val=1)

                def lookups(half, window, seen, filled, used):
                    for q in range(LOOKUP_FILLS):
                        pe.wait_ge(used, seen if q < 2 else seen + (q - 1))
                        pe.sem_inc(lookups_begun, 1)
                        for k in range(4 * q, min(4 * q + 4, GROUP)):
                            mm = pe.matmul(bank[LOOKUP_BANKS[q % 2]][:, k % 4 * P:(k % 4 + 1) * P], etype_hot[:, half, k * P:(k + 1) * P],
                                           S[3][INVERSE, window], start=True, stop=True)
                        mm.then_inc(filled, 1)

                def prepare(conv, i, half):
                    if conv != 1:
                        return
                    g = i * 2 + half
                    base = pe.value_load(base_i[0:1, ds(g, 1)], min_val=0, max_val=N_NODES - 1)
                    pe.wait_ge(etype_hot_ready, g + 1)
                    lookups(half, ds(base, P), g * LOOKUP_FILLS, lookup_psum, looked_up)

                def finish(conv, i, half, may_be_wide):
                    g = i * 2 + half
                    seen = GROUPS * conv
                    pe.wait_ge(cursor_free, g + (seen + 2))
                    pe.wait_ge(onehot_ready, g + (seen + 1))
                    for k in range(GROUP):
                        pe.wait_ge(gathered[half][k], i * 16 + 16 * (PAIRS * conv + 1))
                        for f in range(CONV_WIDTH[conv] // P):
                            mm = pe.matmul(bank[f][:, 0:P], message(conv, half, k, f), onehot[:, half, k, :],
                                           start=(k == 0), stop=(k == GROUP - 1))
                        if conv == 0:
                            mm = pe.matmul(bank[COUNT_BANK][0:32, 0:P], typehot[:, half, k, :], onehot[:, half, k, :],
                                           start=(k == 0), stop=(k == GROUP - 1))
                    mm.then_inc(sums_psum, 1)
                    if not may_be_wide:
                        return
                    with pe.If(wide):
                        with pe.Fori(1, NODE_TILES) as j:
                            step = g * (NODE_TILES - 1) + j
                            pe.wait_ge(wide_onehot, step + seen * (NODE_TILES - 1))
                            if conv == 1:
                                lookups(half, ds(j * P, P), (step - 1) * LOOKUP_FILLS, wide_lookup, wide_looked_up)
                            for f in range(CONV_WIDTH[conv] // P):
                                for k in range(GROUP):
                                    mm = pe.matmul(bank[WIDE_BANK][:, f * P:(f + 1) * P], message(conv, half, k, f), onehot[:, half, k, :],
                                                   start=(k == 0), stop=(k == GROUP - 1))
                            if conv == 0:
                                for k in range(GROUP):
                                    mm = pe.matmul(bank[WIDE_BANK][0:32, 2 * P:3 * P], typehot[:, half, k, :], onehot[:, half, k, :],
                                                   start=(k == 0), stop=(k == GROUP - 1))
                            mm.then_inc(wide_psum, 1)

                def degrees(p, c, tiles):
                    seen = (FULL_CHUNKS + 1) * p
                    pe.wait_ge(counts_kept, c + (seen + 1))
                    pe.wait_ge(scaled, c + seen)
                    if p == 1:
                        pe.wait_ge(table_copied[1], c * (CHUNK_TILES * tile_copies(1)))
                    pe.matmul(bank[DEGREE_BANK][:, 0:tiles * P], ones[COUNT, :], chunk_in[COUNT, 1, 0:tiles * P],
                              start=True, stop=True).then_inc(deg_psum, 1)

                def update(p, c, tiles):
                    pe.wait_ge(updated[p], c)
                    if p == 0:
                        pe.wait_ge(scaled, c + 1)
                    for f, terms in enumerate(UPDATE[p]):
                        for n, (w, src) in enumerate(terms):
                            mm = pe.matmul(bank[UPDATE_BANKS[p][f]][:, 0:tiles * P], w, src[:, chunk_cols(c, tiles)],
                                           start=(n == 0), stop=(n == len(terms) - 1))
                    mm.then_inc(update_psum[p], 1)

                def turn(p, c, tiles):
                    pe.wait_ge(updated[p], c + 1)
                    for t in range(tiles):
                        mm = pe.transpose(bank[TURN_BANK[p]][:, t * P:(t + 1) * P], chunk_in[:, 0, t * P:(t + 1) * P], ident[:, :])
                    mm.then_inc(turned, 1)

                def embed(c, tiles):
                    pe.matmul(bank[EMB_BANK][:, 0:tiles * P], emb[NTYPE, :], chunk_in[NTYPE, 1, 0:tiles * P],
                              start=True, stop=True).then_inc(emb_psum, 1)

                def turn_back(c, tiles):
                    pe.wait_ge(normed_ready, c + 1)
                    for t in range(tiles):
                        mm = pe.transpose(bank[BACK_BANK][:, t * P:(t + 1) * P], normed[:, t, :], ident[:, :])
                    mm.then_inc(turned_back, 1)

                def table(p, c, t):
                    copies = tile_copies(p)
                    pe.wait_ge(chunk_kept[p], c * chunk_copies(p) + chunk_copies(p))
                    if p == 1:
                        pe.wait_ge(norm_kept, c + 1)
                        pe.wait_ge(emb_kept, c + 1)
                    if p:
                        pe.wait_ge(table_w_in, 16 * [0, 2, 4, 5][p])
                    for m, (at, size) in enumerate(cuts(TABLE_COLS[p])):
                        n = t * copies + m
                        pe.wait_ge(table_copied[p], c * (CHUNK_TILES * copies) + max(0, n - 1))
                        halves = len(TABLE_IN[p])
                        for h in range(halves):
                            mm = pe.matmul(bank[TABLE_BANKS[n % 2]][:, 0:size], chunk_in[:, h, t * P:(t + 1) * P], table_weights(p, h, at, size),
                                           start=(h == 0), stop=(h == halves - 1))
                        mm.then_inc(table_psum[p], 1)

                def chunk_slice(conv, c, slot, tiles):
                    at = slot - CHUNK_SLOT
                    if at == 0:
                        if conv < 2:
                            degrees(conv, c, tiles)
                        update(conv, c, tiles)
                    if at == 1 and conv in (1, 4):
                        turn(conv, c, tiles)
                    if at == 1 and conv == 1:
                        embed(c, tiles)
                    if at == 2 and conv == 1:
                        turn_back(c, tiles)
                    if conv < 4:
                        for t in TILE_SLOTS[conv].get(at, []):
                            if t < tiles:
                                table(conv, c, t)

                for conv in range(CONVS):
                    prepare(conv, 0, 0)
                    with pe.If(ordered):
                        with pe.Fori(0, STRETCH_PAIRS) as i:
                            for half in range(2):
                                prepare(conv, i + half, 1 - half)
                                finish(conv, i, half, False)
                        with pe.Fori(1, STRETCHES) as o:
                            for slot in range(SLOTS):
                                prepare(conv, o * STRETCH_PAIRS + (slot + 1) // 2, (slot + 1) % 2)
                                finish(conv, o * STRETCH_PAIRS + slot // 2, slot % 2, False)
                                chunk_slice(conv, o - 1, slot, CHUNK_TILES)
                    with pe.Else():
                        with pe.Fori(0, STRETCHES * STRETCH_PAIRS) as i:
                            for half in range(2):
                                prepare(conv, i + half, 1 - half)
                                finish(conv, i, half, True)
                    for g in range(STRETCHES * SLOTS, GROUPS):
                        if g + 1 < GROUPS:
                            prepare(conv, (g + 1) // 2, (g + 1) % 2)
                        finish(conv, g // 2, g % 2, True)
                    with pe.If(ordered):
                        pe.sem_inc(branches_joined, 1)
                    with pe.Else():
                        with pe.Fori(0, FULL_CHUNKS - 1) as c:
                            for slot in range(CHUNK_SLOT, SLOTS):
                                chunk_slice(conv, c, slot, CHUNK_TILES)
                    for c, tiles in ((FULL_CHUNKS - 1, CHUNK_TILES), (FULL_CHUNKS, LAST_TILES)):
                        for slot in range(CHUNK_SLOT, SLOTS):
                            chunk_slice(conv, c, slot, tiles)

            @block.vector
            def _(vec):
                def step(op, n):
                    op.then_inc(vec_prep, 1)
                    vec.wait_ge(vec_prep, n)

                vec.wait_ge(consts, 7)
                step(vec.tensor_copy(iota_f[:, :], iota_i[:, :]), 1)
                step(vec.tensor_copy(lane_f[:, :], lane_i[:, :]), 2)
                step(vec.tensor_scalar(ident[:, :], iota_f[:, :], lane_f[:, 0:1], None, ALU.is_equal), 3)
                vec.wait_ge(edges_in, 160)
                vec.wait_ge(types_padded, 32)
                for n in range(3):
                    step(vec.tensor_copy(edge_f[n], edge_i[n]), 4 + n)
                step(vec.tensor_scalar(S[3][NTYPE, 0:N_NODES], ntype_i, lane_f[NTYPE, 1:2], None, ALU.is_equal), 7)
                step(vec.tensor_reduce(tile_low[:, :], edge_f[0], AX.X, ALU.min), 8)
                step(vec.scalar_tensor_tensor(out=onehot[:, 0, :, :], in0=edge_f[0], scalar=float(NO_NODE), in1=edge_f[0], op0=ALU.is_lt, op1=ALU.mult), 9)
                step(vec.tensor_reduce(tile_high[:, :], onehot[:, 0, :, :], AX.X, ALU.max), 10)
                by_group = lambda v: v[:, 0:EDGE_TILES].rearrange("p (g k) -> p g k", k=GROUP)
                vec.wait_ge(bounds_in, 16)
                step(vec.tensor_reduce(base_f[:, :], by_group(bounds), AX.X, ALU.min), 11)
                vec.wait_ge(bounds_in, 32)
                step(vec.tensor_reduce(high_f[:, :], by_group(bounds), AX.X, ALU.max), 12)
                step(vec.tensor_copy(limit_f[:, :], limit_i[:, :]), 13)
                step(vec.tensor_tensor(limit_f[:, :], base_f[:, CHUNK_SLOT:CHUNK_SLOT + STRETCHES * SLOTS], limit_f[:, :], ALU.subtract), 14)
                step(vec.tensor_reduce(ordered_f[:, :], limit_f[:, :], AX.X, ALU.min), 15)
                step(vec.tensor_tensor(span_f[:, :], high_f[:, :], base_f[:, :], ALU.subtract), 16)
                step(vec.tensor_reduce(wide_f[:, :], span_f[:, :], AX.X, ALU.max), 17)
                step(vec.tensor_scalar(wide_f[:, :], wide_f[:, :], float(P - 1), None, ALU.is_gt), 18)
                step(vec.tensor_scalar(narrow_f[:, :], wide_f[:, :], -1.0, 1.0, ALU.mult, ALU.add), 19)
                step(vec.tensor_scalar(ordered_f[:, :], ordered_f[:, :], 0.0, narrow_f[:, 0:1], ALU.is_ge, ALU.mult), 20)
                step(vec.tensor_scalar(base_f[:, :], base_f[:, :], narrow_f[:, 0:1], None, ALU.mult), 21)
                step(vec.tensor_copy(base_i[:, :], base_f[0:1, :]), 22)
                step(vec.tensor_copy(wide_i[:, :], wide_f[0:1, :]), 23)
                step(vec.tensor_copy(ordered_i[:, :], ordered_f[0:1, :]), 24)
                vec.wait_ge(prep_kept, EDGE_FILLS)
                step(vec.tensor_tensor(by_group(rel_all), by_group(dst_T), base_f[:, :].unsqueeze(2).broadcast_to([P, GROUPS, GROUP]), ALU.subtract), 25)
                step(vec.tensor_copy(row_all[:, :], src_T[:, 0:EDGE_TILES]), 26)
                vec.wait_ge(prep_kept, len(FILLS))
                step(vec.memset(S[1][:, :], 0.0), 27)
                step(vec.memset(S[2][:, :], 0.0), VEC_PREPARED)
                for n in range(2):
                    vec.sem_inc(cursor_free, 1)

                ordered = vec.value_load(ordered_i[0:1, 0:1], min_val=0, max_val=1)
                wide = vec.value_load(wide_i[0:1, 0:1], min_val=0, max_val=1)

                def build_onehots(conv, half, rel, signal):
                    for k in range(GROUP):
                        weight = dict(scalar2=weight_cur[:, half, k:k + 1], op1=ALU.mult) if conv >= 2 else dict(scalar2=None)
                        op = vec.tensor_scalar(onehot[:, half, k, :], iota_f[:, :], scalar1=rel(k), op0=ALU.is_equal, **weight)
                    op.then_inc(signal, 1)

                def add_sums(conv, source, window):
                    for f, sums in enumerate(SUMS[conv]):
                        op = vec.tensor_tensor(sums[:, window], sums[:, window], source[f], ALU.add)
                    if conv == 0:
                        op = vec.tensor_tensor(S[3][SUMMED, window], S[3][SUMMED, window], source[-1], ALU.add)
                    return op

                def lookups(half, into, seen, filled, used):
                    for q in range(LOOKUP_FILLS):
                        vec.wait_ge(filled, seen + (q + 1))
                        for k in range(4 * q, min(4 * q + 4, GROUP)):
                            at = bank[LOOKUP_BANKS[q % 2]][:, k % 4 * P:(k % 4 + 1) * P]
                            op = vec.tensor_tensor_reduce(at, at, onehot[:, half, k, :], 1.0, 0.0, ALU.mult, ALU.add, into[:, k:k + 1])
                        op.then_inc(used, 1)

                def prepare(conv, i, half):
                    g = i * 2 + half
                    seen = GROUPS * conv
                    if conv == 1:
                        vec.wait_ge(etype_in, g * 16 + 16)
                        vec.tensor_scalar(etype_hot[:, half, :], etype_row, lane_f[INVERSE, 0:1], None, ALU.is_equal).then_inc(etype_hot_ready, 1)
                    vec.wait_ge(cursor_ready, g * CURSORS + CURSORS * (seen + 1))
                    if conv == 0:
                        vec.tensor_tensor(typehot[:, half, :, :], iota_f[:, 0:32].unsqueeze(1).broadcast_to([P, GROUP, 32]),
                                          weight_cur[:, half, :].unsqueeze(2).broadcast_to([P, GROUP, 32]), ALU.is_equal)
                    build_onehots(conv, half, lambda k: rel_cur[:, half, k:k + 1], onehot_ready)
                    if conv == 1:
                        vec.wait_ge(onehot_ready, g + (seen + 1))
                        lookups(half, part[:, half, :], g * LOOKUP_FILLS, lookup_psum, looked_up)

                def finish(conv, i, half, may_be_wide):
                    g = i * 2 + half
                    seen = GROUPS * conv
                    base = vec.value_load(base_i[0:1, ds(g, 1)], min_val=0, max_val=N_NODES - 1)
                    if may_be_wide:
                        with vec.If(wide):
                            wide_windows(conv, g, half, seen)
                    if conv == 1:
                        vec.wait_ge(looked_up, g * LOOKUP_FILLS + LOOKUP_FILLS)
                        rows, types = row_all[:, ds(g * GROUP, GROUP)], type_all[:, ds(g * GROUP, GROUP)]
                        vec.scalar_tensor_tensor(out=rows, in0=rows, scalar=float(RELATIONS), in1=types, op0=ALU.mult, op1=ALU.add).then_inc(rel_rows_made, 1)
                        vec.wait_ge(rel_rows_made, g + 1)
                        vec.sem_inc(weighed, 1)
                        vec.tensor_copy(weight_all[:, ds(g * GROUP, GROUP)], part[:, half, :])
                    vec.wait_ge(sums_psum, g + (seen + 1))
                    source = [bank[f][:, 0:P] for f in range(CONV_WIDTH[conv] // P)] + [bank[COUNT_BANK][0:32, 0:P]]
                    add_sums(conv, source, ds(base, P)).then_inc(cursor_free, 1)
                    vec.wait_ge(cursor_free, g + (seen + 3))

                def wide_windows(conv, g, half, seen):
                    vec.wait_ge(sums_psum, g + (seen + 1))
                    if conv == 1:
                        vec.wait_ge(looked_up, g * LOOKUP_FILLS + LOOKUP_FILLS)
                    rel_steps = NODE_TILES
                    vec.tensor_copy(rel_wide[:, :], rel_cur[:, half, :]).then_inc(wide_rel, 1)
                    with vec.Fori(1, NODE_TILES) as j:
                        done = g * (NODE_TILES - 1) + j + seen * (NODE_TILES - 1)
                        vec.wait_ge(wide_rel, g * rel_steps + j + seen * rel_steps)
                        vec.tensor_scalar(rel_wide[:, :], rel_wide[:, :], -float(P), None, ALU.add).then_inc(wide_rel, 1)
                        vec.wait_ge(wide_rel, g * rel_steps + j + (seen * rel_steps + 1))
                        build_onehots(conv, half, lambda k: rel_wide[:, k:k + 1], wide_onehot)
                        vec.wait_ge(wide_onehot, done)
                        if conv == 1:
                            lookups(half, part_wide, (done - 1) * LOOKUP_FILLS, wide_lookup, wide_looked_up)
                            vec.wait_ge(wide_looked_up, done * LOOKUP_FILLS)
                            vec.tensor_tensor(part[:, half, :], part[:, half, :], part_wide[:, :], ALU.add).then_inc(wide_part, 1)
                            vec.wait_ge(wide_part, g * (NODE_TILES - 1) + j)
                        vec.wait_ge(wide_psum, done)
                        source = [bank[WIDE_BANK][:, f * P:(f + 1) * P] for f in range(CONV_WIDTH[conv] // P)] + [bank[WIDE_BANK][0:32, 2 * P:3 * P]]
                        add_sums(conv, source, ds(j * P, P))

                def invert_counts(c, tiles):
                    cols = chunk_cols(c, tiles)
                    vec.tensor_copy(S[3][COUNT, cols], S[3][SUMMED, cols]).then_inc(inverted, 1)
                    vec.wait_ge(inverted, c * 3 + 1)
                    vec.tensor_scalar(S[3][INVERSE, cols], S[3][INVERSE, cols], 1.0, None, ALU.max).then_inc(inverted, 1)
                    vec.wait_ge(inverted, c * 3 + 2)
                    vec.sem_inc(inverting, 1)
                    vec.reciprocal(S[3][INVERSE, cols], S[3][INVERSE, cols]).then_inc(inverted, 1)

                def scale_by_degree(p, c, tiles):
                    seen = (FULL_CHUNKS + 1) * p
                    inv = inv_deg[:, 0:tiles * P]
                    vec.wait_ge(deg_psum, c + (seen + 1))
                    vec.tensor_scalar(inv, bank[DEGREE_BANK][:, 0:tiles * P], 1.0, None, ALU.max).then_inc(deg_step, 1)
                    vec.wait_ge(deg_step, c * 2 + (2 * seen + 1))
                    vec.reciprocal(inv, inv).then_inc(deg_step, 1)
                    vec.wait_ge(deg_step, c * 2 + (2 * seen + 2))
                    sums = S[1 + p][:, chunk_cols(c, tiles)]
                    vec.tensor_tensor(sums, sums, inv, ALU.mult).then_inc(scaled, 1)

                def update(p, c, tiles):
                    cols = chunk_cols(c, tiles)
                    psum = [bank[b][:, 0:tiles * P] for b in UPDATE_BANKS[p]]
                    vec.wait_ge(update_psum[p], c + 1)
                    if p == 0:
                        vec.tensor_scalar(S[1][:, cols], psum[0], BIAS[0][0], 0.0, ALU.add, ALU.max).then_inc(updated[p], 1)
                        return
                    if p == 1:
                        vec.wait_ge(scaled, c + (FULL_CHUNKS + 2))
                    for f, sums in enumerate(SUMS[p]):
                        op = vec.scalar_tensor_tensor(out=sums[:, cols], in0=psum[f], scalar=BIAS[p][f], in1=sums[:, cols], op0=ALU.add, op1=ALU.add)
                    op.then_inc(update_step[p], 1)
                    vec.wait_ge(update_step[p], c + 1)
                    if p == 1:
                        vec.wait_ge(table_psum[1], c * (CHUNK_TILES * tile_copies(1)))
                    fixed = chunk_in[:, 0, 0:tiles * P]
                    for f, sums in enumerate(SUMS[p]):
                        if p == 1:
                            op = vec.tensor_tensor(fixed, sums[:, cols], S[0][:, cols], ALU.add)
                        elif p == 4:
                            op = vec.scalar_tensor_tensor(out=fixed, in0=sums[:, cols], scalar=0.0, in1=S[0][:, cols], op0=ALU.max, op1=ALU.add)
                        else:
                            op = vec.tensor_scalar(sums[:, cols], sums[:, cols], 0.0, None, ALU.max)
                    op.then_inc(updated[p], 1)

                def norm(which, c, tiles):
                    seen = (FULL_CHUNKS + 1) * which
                    source = bank[TURN_BANK[(1, 4)[which]]]
                    vec.wait_ge(turned, c + (seen + 1))
                    for t in range(tiles):
                        op = vec.bn_stats(stats[:, t, :], source[:, t * P:(t + 1) * P])
                    op.then_inc(norm_step, 1)
                    vec.wait_ge(norm_step, c * 3 + (seen * 3 + 1))
                    vec.sem_inc(moments_begun, 1)
                    for t in range(tiles):
                        op = vec.bn_aggr(moments[:, t, :], stats[:, t, :])
                    op.then_inc(norm_step, 1)
                    vec.wait_ge(deviation, c + (seen + 1))
                    vec.reciprocal(rstd[:, 0:tiles], rstd[:, 0:tiles]).then_inc(norm_step, 1)
                    vec.wait_ge(norm_step, c * 3 + (seen * 3 + 3))
                    if which == 0:
                        vec.wait_ge(turned_back, c)
                    else:
                        vec.wait_ge(out_stored, c * 16)
                    for t in range(tiles):
                        op = vec.tensor_scalar(normed[:, t, :], source[:, t * P:(t + 1) * P], moments[:, t, 0:1], rstd[:, t:t + 1], ALU.subtract, ALU.mult)
                    op.then_inc(normed_ready, 1)

                def zero(p, c, tiles):
                    width = tiles * P if tiles == CHUNK_TILES else ACC_COLS - FULL_CHUNKS * CHUNK
                    if p == 1:
                        vec.wait_ge(updated[1], c + 1)
                        vec.wait_ge(counts_kept, c + (FULL_CHUNKS + 2))
                    vec.sem_inc(zeroing, 1)
                    for s in SUMS[p + 1]:
                        place = s[:, ds(c * CHUNK, width)]
                        op = vec.tensor_copy(place, zeros[:, 0:1].broadcast_to([P, width]))
                    op.then_inc(zeroed, 1)

                def chunk_slice(conv, c, slot, tiles):
                    at = slot - CHUNK_SLOT
                    if at == 0:
                        if conv == 0:
                            invert_counts(c, tiles)
                        if conv < 2:
                            scale_by_degree(conv, c, tiles)
                        update(conv, c, tiles)
                        if 1 <= conv <= 3:
                            zero(conv, c, tiles)
                    if at == 1 and conv in (1, 4):
                        norm(conv // 4, c, tiles)

                for conv in range(CONVS):
                    if conv >= 2:
                        vec.wait_ge(zeroed, (FULL_CHUNKS + 1) * (conv - 1))
                    prepare(conv, 0, 0)
                    with vec.If(ordered):
                        with vec.Fori(0, STRETCH_PAIRS) as i:
                            for half in range(2):
                                prepare(conv, i + half, 1 - half)
                                finish(conv, i, half, False)
                        with vec.Fori(1, STRETCHES) as o:
                            for slot in range(SLOTS):
                                prepare(conv, o * STRETCH_PAIRS + (slot + 1) // 2, (slot + 1) % 2)
                                finish(conv, o * STRETCH_PAIRS + slot // 2, slot % 2, False)
                                chunk_slice(conv, o - 1, slot, CHUNK_TILES)
                    with vec.Else():
                        with vec.Fori(0, STRETCHES * STRETCH_PAIRS) as i:
                            for half in range(2):
                                prepare(conv, i + half, 1 - half)
                                finish(conv, i, half, True)
                    for g in range(STRETCHES * SLOTS, GROUPS):
                        if g + 1 < GROUPS:
                            prepare(conv, (g + 1) // 2, (g + 1) % 2)
                        finish(conv, g // 2, g % 2, True)
                    with vec.If(ordered):
                        vec.sem_inc(branches_joined, 1)
                    with vec.Else():
                        with vec.Fori(0, FULL_CHUNKS - 1) as c:
                            for slot in range(CHUNK_SLOT, SLOTS):
                                chunk_slice(conv, c, slot, CHUNK_TILES)
                    for c, tiles in ((FULL_CHUNKS - 1, CHUNK_TILES), (FULL_CHUNKS, LAST_TILES)):
                        for slot in range(CHUNK_SLOT, SLOTS):
                            chunk_slice(conv, c, slot, tiles)


_INS = ['x', 'src', 'dst', 'edge_type_5', 'node_type_3', 'L0_gnn_W1l', 'L0_gnn_b1l', 'L0_gnn_W1r', 'L0_gnn_W2l', 'L0_gnn_b2l',
        'L0_gnn_W2r', 'L1_gnn_node_emb', 'L1_gnn_W1', 'L1_gnn_root1', 'L1_gnn_b1', 'L1_gnn_W2', 'L1_gnn_root2', 'L1_gnn_b2',
        'L1_gnn_W3', 'L1_gnn_root3', 'L1_gnn_b3']


def kernel(**inputs):
    import numpy as np
    import concourse.bacc as bacc
    from concourse import mybir as mb
    from concourse.bass_utils import run_bass_kernel_spmd as run

    nc = bacc.Bacc("TRN2", target_bir_lowering=False, num_devices=1)
    arrays, aps = {}, {}
    for name in _INS:
        v = np.ascontiguousarray(inputs[name])
        arrays[f"in_{name}"] = v
        aps[name] = nc.dram_tensor(f"in_{name}", v.shape, mb.dt.from_np(v.dtype), kind="ExternalInput").ap()
    out = nc.dram_tensor("out", (N_NODES, FEAT), mb.dt.float32, kind="ExternalOutput").ap()
    resnorm_gnn(nc, aps, out)
    return run(nc, [arrays], core_ids=[0]).results[0]["out"]
```

```python
from contextlib import ExitStack

import concourse.bass as bass
from concourse import mybir

P = 128
N_NODES = 6250
N_EDGES = 206250
FEAT = 128
WIDE = 256
RELATIONS = 5
NODE_TYPES = 3
EPS = 1e-5

NODE_TILES = -(-N_NODES // P)
NODES_PADDED = NODE_TILES * P
CHUNK_TILES = 4
CHUNK = CHUNK_TILES * P
LAST_CHUNKS = [3, 2]
FULL_CHUNKS = (NODE_TILES - sum(LAST_CHUNKS)) // CHUNK_TILES
CHUNKS = FULL_CHUNKS + len(LAST_CHUNKS)
LAST_FIRST = NODE_TILES - LAST_CHUNKS[-1]
assert FULL_CHUNKS * CHUNK_TILES + sum(LAST_CHUNKS) == NODE_TILES
WINDOWS = NODE_TILES
ACC_COLS = NODES_PADDED + P

EDGE_TILES = -(-N_EDGES // P)
GROUP = 13
GROUPS = EDGE_TILES // GROUP
assert GROUPS * GROUP == EDGE_TILES and GROUPS % 2 == 0
PAIRS = GROUPS // 2
SLOTS = 10
STRETCHES = 12
CHUNK_SLOT = 3
STRETCH_PAIRS = SLOTS // 2
LAST_GROUPS = range(STRETCHES * SLOTS, GROUPS)
assert len(LAST_GROUPS) == 4 and STRETCHES - 1 == FULL_CHUNKS
SLICES = SLOTS - CHUNK_SLOT
UPDATE_AT = [0, 1, 0, 0, 0]
TURN_AT = [at + 1 for at in UPDATE_AT]
EDGE_BLOCKS = -(-EDGE_TILES // P)
FULL_BLOCKS = EDGE_TILES // P
LAST_ROWS = N_EDGES // P - FULL_BLOCKS * P
LAST_NODES = N_NODES - (NODE_TILES - 1) * P
LAST_EDGES = N_EDGES % P
NO_NODE = 1000000

CONV_WIDTH = [FEAT, FEAT, WIDE, FEAT, FEAT]
CONVS = len(CONV_WIDTH)
BAND = 32


def resnorm_gnn(nc, a, out):
    f32, i32, bf16 = mybir.dt.float32, mybir.dt.int32, mybir.dt.bfloat16
    ALU, ACT, AX = mybir.AluOpType, mybir.ActivationFunctionType, mybir.AxisListType
    ds = bass.ds

    table_h = nc.dram_tensor("table_h", (NODES_PADDED, FEAT), f32).ap()
    table_1 = nc.dram_tensor("table_1", (NODES_PADDED, RELATIONS * WIDE), f32).ap()
    table_2 = nc.dram_tensor("table_2", (NODES_PADDED, RELATIONS * FEAT), f32).ap()
    table_3 = nc.dram_tensor("table_3", (NODES_PADDED, RELATIONS * FEAT), f32).ap()
    per_relation = lambda t: t.rearrange("n (r f) -> (n r) f", r=RELATIONS)
    GATHERED = [a["x"], table_h, per_relation(table_1), per_relation(table_2), per_relation(table_3)]
    STORED = [table_h, table_1, table_2, table_3]
    bounds_d = nc.dram_tensor("bounds_d", (2, EDGE_BLOCKS * P), f32).ap()
    types_d = nc.dram_tensor("types_d", (1, EDGE_TILES * P), i32).ap()

    ctx = ExitStack()
    with ctx:
        sb = lambda name, shape, dt=f32: ctx.enter_context(nc.sbuf_tensor(name, shape, dt))
        sem = lambda name: ctx.enter_context(nc.semaphore(name))

        S = [sb(f"S{n}", [P, ACC_COLS]) for n in range(4)]
        SUMMED, INVERSE, COUNT, NTYPE = slice(0, 32), slice(0, RELATIONS), slice(32, 64), slice(64, 64 + NODE_TYPES)
        msgs = sb("msgs", [P, 2 * GROUP * WIDE])
        onehot = sb("onehot", [P, 2, GROUP, P])
        row_all = sb("row_all", [P, EDGE_TILES], i32)
        rel_all = sb("rel_all", [P, EDGE_TILES])
        type_all = sb("type_all", [P, EDGE_TILES])
        weight_all = type_all
        row_cur = sb("row_cur", [P, 2, GROUP], i32)
        rel_cur = sb("rel_cur", [P, 2, GROUP])
        weight_cur = sb("weight_cur", [P, 2, GROUP])
        rel_wide = sb("rel_wide", [P, GROUP])
        typehot = sb("typehot", [P, 2, GROUP, 32])
        part = sb("part", [P, 2, GROUP])
        part_wide = sb("part_wide", [P, GROUP])
        base_f = sb("base_f", [P, GROUPS])
        wide_f = sb("wide_f", [P, 1])
        narrow_f = sb("narrow_f", [P, 1])
        base_i = sb("base_i", [1, GROUPS], i32)
        wide_i = sb("wide_i", [1, 1], i32)
        tile_bounds = sb("tile_bounds", [P, 2, EDGE_BLOCKS])
        iota_f = sb("iota_f", [P, P])
        lane_i = sb("lane_i", [P, 2], i32)
        lane_f = sb("lane_f", [P, 2])
        ident = sb("ident", [P, P])
        ones = sb("ones", [P, P])
        eps = sb("eps", [P, 1])
        zeros = sb("zeros", [P, 1])
        bias = sb("bias", [P, 6])
        w_T = sb("w_T", [P, 4, P])
        emb = sb("emb", [P, FEAT])
        emb_T = sb("emb_T", [P, 3, BAND])
        table_w = sb("table_w", [P, 2 * RELATIONS * WIDE])
        root1 = sb("root1", [P, 2, WIDE])
        root2 = sb("root2", [P, 2, FEAT])
        root3 = sb("root3", [P, FEAT])
        chunk_in = sb("chunk_in", [P, 2, CHUNK])
        type_bands = sb("type_bands", [3 * BAND, CHUNK], bf16)
        inv_deg = sb("inv_deg", [P, CHUNK])
        stats = sb("stats", [P, CHUNK_TILES, 6])
        moments = sb("moments", [P, CHUNK_TILES, 2])
        rstd = sb("rstd", [P, CHUNK_TILES])
        normed = sb("normed", [P, CHUNK_TILES, P])
        stage = sb("stage", [P, 2, RELATIONS * WIDE])
        early = stage[:, :, :].rearrange("p s f -> p (s f)")
        limit_i = early[:, 0:GROUPS].bitcast(i32)
        limit_f = early[:, P:P + GROUPS]
        high_f = early[:, 2 * P:2 * P + GROUPS]
        span_f = early[:, 3 * P:3 * P + GROUPS]
        iota_i = early[:, 4 * P:5 * P].bitcast(i32)
        ordered_f = sb("ordered_f", [P, 1])
        ordered_i = sb("ordered_i", [1, 1], i32)
        etype_row_t = sb("etype_row", [P, GROUP * P], i32)

        bank = [ctx.enter_context(nc.psum_tensor(f"bank{n}", [P, 512], f32)) for n in range(8)]

        x_behind = msgs[:, 2 * GROUP * FEAT:4 * GROUP * FEAT].rearrange("p (t f) -> p t f", f=P)
        x_in_table = table_w[:, :].rearrange("p (t f) -> p t f", f=P)
        X_BEHIND, X_IN_TABLE = 2 * GROUP, 2 * RELATIONS * WIDE // P
        X_PLACES = [(x_behind, 0, X_BEHIND), (x_in_table, X_BEHIND, X_IN_TABLE), (normed, X_BEHIND + X_IN_TABLE, NODE_TILES - X_BEHIND - X_IN_TABLE)]

        def x_tile(t):
            place, first = [(place, first) for place, first, count in X_PLACES if first <= t][-1]
            return place[:, t - first, :]
        edge_cols = EDGE_BLOCKS * P
        edge_f = [S[2][:, n * edge_cols:(n + 1) * edge_cols].rearrange("p (b c) -> p b c", c=P) for n in range(3)]
        edge_i = [v.bitcast(i32) for v in edge_f]
        src_T = S[1][:, 0:edge_cols]
        dst_T = S[1][:, edge_cols:2 * edge_cols]
        ntype_i = S[3][NTYPE, 0:N_NODES].bitcast(i32)
        etype_row = etype_row_t[INVERSE, :]
        w_raw = etype_row_t[:, 0:4 * P].bitcast(f32).rearrange("p (n f) -> p n f", n=4)
        etype_hot = msgs[INVERSE, 2 * GROUP * FEAT:2 * GROUP * (FEAT + P)].rearrange("p (h c) -> p h c", h=2)
        bounds = onehot[:, :, :, :].rearrange("p h k c -> p h (k c)")

        def message(conv, half, k, f):
            w = CONV_WIDTH[conv]
            at = (half * GROUP + k) * w
            return msgs[:, at + f * P:at + (f + 1) * P]

        SUMS = [[S[1]], [S[2]], [S[2], S[3]], [S[1]], [S[2]]]

        UPDATE = [
            [[(w_T[:, 0, :], S[1]), (w_T[:, 1, :], S[0])]],
            [[(w_T[:, 3, :], S[1])]],
            [[(root1[:, 0, f * P:(f + 1) * P], S[0]), (root1[:, 1, f * P:(f + 1) * P], S[1])] for f in range(2)],
            [[(root2[:, 0, :], S[2]), (root2[:, 1, :], S[3])]],
            [[(root3[:, :], S[1])]],
        ]
        BIAS = [[bias[:, 0:1]], [bias[:, 1:2]], [bias[:, 2:3], bias[:, 3:4]], [bias[:, 4:5]], [bias[:, 5:6]]]
        TABLE_IN = [[S[1]], [S[0]], [S[2], S[3]], [S[1]]]
        WEIGHT_HALVES = [1, 2, 2, 1]
        TABLE_COLS = [FEAT, RELATIONS * WIDE, RELATIONS * FEAT, RELATIONS * FEAT]

        def table_weights(p, h, at, n):
            return w_T[:, 2, :] if p == 0 else table_w[:, h * TABLE_COLS[p] + at:h * TABLE_COLS[p] + at + n]

        emb_weights = table_w[:, TABLE_COLS[1]:2 * TABLE_COLS[1]]
        emb_table = table_w[0:3 * BAND, TABLE_COLS[1]:TABLE_COLS[1] + TABLE_COLS[1] // 2].bitcast(bf16)
        EMB_BANKS = (3, 4, 3)

        cuts = lambda n: [(c, min(512, n - c)) for c in range(0, n, 512)]
        is_last = lambda c: isinstance(c, int) and c == CHUNKS - 1
        first_tile = lambda c: LAST_FIRST if is_last(c) else c * CHUNK_TILES
        chunk_cols = lambda c, tiles: ds(first_tile(c) * P, tiles * P)
        tile_rows = lambda c, t: ds(first_tile(c) * P + t * P, P)
        chunk_copies = lambda p: 4 if p == 1 else len(TABLE_IN[p])
        TILE_SLOTS = [{1: [0], 2: [1], 3: [2], 4: [3]}] * 4
        TILE_SLOTS[1] = {3: [0], 4: [1, 2], 5: [3]}
        COUNT_BANK, LOOKUP_BANKS, WIDE_BANK = 2, (3, 4, 1, 2), 7
        DEGREE_BANK, EMB_BANK, BACK_BANK = 7, 6, 5
        UPDATE_BANKS = [(1,), (7,), (2, 3), (2,), (2,)]
        TURN_BANK = [None, 7, None, None, 3]
        TABLE_BANKS = (5, 6)
        LOOKUP_FILLS = -(-GROUP // 4)

        padded, dst_in, edges_in, types_padded = sem("padded"), sem("dst_in"), sem("edges_in"), sem("types_padded")
        x_in, w_in, small_in, ntype_in = sem("x_in"), sem("w_in"), sem("small_in"), sem("ntype_in")
        emb_spread, emb_rows_psum, emb_split = sem("emb_spread"), sem("emb_rows_psum"), sem("emb_split")
        bounds_out, bounds_in = sem("bounds_out"), sem("bounds_in")
        table_w_in = sem("table_w_in")
        consts = sem("consts")
        vec_prep = sem("vec_prep")
        prep_psum, prep_kept = sem("prep_psum"), sem("prep_kept")
        inverting = sem("inverting")
        inverted = sem("inverted")
        zeroed = sem("zeroed")
        rel_rows_made, zeroing = sem("rel_rows_made"), sem("zeroing")
        cursor_free, cursor_ready = sem("cursor_free"), sem("cursor_ready")
        lookups_begun = sem("lookups_begun")
        gathers_begun, moments_begun = sem("gathers_begun"), sem("moments_begun")
        gathered = [[sem(f"gathered{h}_{k}") for k in range(GROUP)] for h in range(2)]
        onehot_ready, sums_psum = sem("onehot_ready"), sem("sums_psum")
        etype_in, etype_hot_ready = sem("etype_in"), sem("etype_hot_ready")
        lookup_psum, looked_up, weighed = sem("lookup_psum"), sem("looked_up"), sem("weighed")
        wide_lookup, wide_looked_up = sem("wide_lookup"), sem("wide_looked_up")
        wide_onehot, wide_psum, wide_rel, wide_part = sem("wide_onehot"), sem("wide_psum"), sem("wide_rel"), sem("wide_part")
        deg_psum, deg_step, scaled = sem("deg_psum"), sem("deg_step"), sem("scaled")
        update_psum = [sem(f"update_psum{p}") for p in range(CONVS)]
        update_step = [sem(f"update_step{p}") for p in range(CONVS)]
        updated = [sem(f"updated{p}") for p in range(CONVS)]
        counts_kept = sem("counts_kept")
        chunk_kept = [sem(f"chunk_kept{p}") for p in range(4)]
        turned, deviation, norm_step, normed_ready = sem("turned"), sem("deviation"), sem("norm_step"), sem("normed_ready")
        turned_back, norm_kept = sem("turned_back"), sem("norm_kept")
        emb_psum, emb_kept = sem("emb_psum"), sem("emb_kept")
        table_psum = [sem(f"table_psum{p}") for p in range(4)]
        table_copied = [sem(f"table_copied{p}") for p in range(4)]
        row_stored = [[sem(f"row_stored{p}_{s}") for s in range(2)] for p in range(4)]
        out_stored = sem("out_stored")

        CURSORS = 3
        freed = lambda conv: 2 + GROUPS * (conv + 1)
        stored_before = lambda c, place: FULL_CHUNKS * 2 + (2 - place) if is_last(c) else c * 2
        stores_in_all = lambda place: stored_before(CHUNKS - 1, place) + 1
        tile_copies = lambda p: len(cuts(TABLE_COLS[p]))
        BOUNDED, EDGES_IN_FLOAT, ROWS_READY, VEC_PREPARED = 7, 9, 10, 25
        SMALL_LOADS = 11
        X_LOADS = 1 + sum(-(-min(count, NODE_TILES - 1 - first) // 4) for place, first, count in X_PLACES)
        SPLIT_STEPS = 7
        FILLS = [("w", 0, 4)]
        FILLS += [(n, b, min(4, EDGE_BLOCKS - b)) for n in range(3) for b in range(0, EDGE_BLOCKS, 4)]
        EDGE_FILLS = len(FILLS)
        FILLS += [("x", t, min(4, NODE_TILES - t)) for t in range(0, NODE_TILES, 4)]

        with nc.Block() as block:

            @block.sync
            def _(sp):
                sp.wait_ge(padded, 4)
                full = FULL_BLOCKS * P * P
                whole = full + LAST_ROWS * P
                for n, (name, landed) in enumerate([("dst", dst_in), ("src", edges_in), ("edge_type_5", edges_in)]):
                    e = a[name]
                    sp.dma_start(edge_i[n][:, 0:FULL_BLOCKS, :], e[0:full].rearrange("(b r c) -> r b c", r=P, c=P)).then_inc(landed, 16)
                    sp.dma_start(edge_i[n][0:LAST_ROWS, FULL_BLOCKS, :], e[full:whole].rearrange("(r c) -> r c", c=P)).then_inc(landed, 16)
                    sp.dma_start(edge_i[n][LAST_ROWS:LAST_ROWS + 1, FULL_BLOCKS, 0:LAST_EDGES], e[whole:N_EDGES].rearrange("(o c) -> o c", o=1)).then_inc(landed, 16)
                sp.dma_start(types_d[0:1, N_EDGES:EDGE_TILES * P], edge_i[2][LAST_ROWS:LAST_ROWS + 1, FULL_BLOCKS, LAST_EDGES:P]).then_inc(types_padded, 16)
                sp.dma_start(types_d[0, 0:N_EDGES].rearrange("(r c) -> r c", c=1650), a["edge_type_5"].rearrange("(r c) -> r c", c=1650)).then_inc(types_padded, 16)
                for n, name in enumerate(["L0_gnn_W1l", "L0_gnn_W1r", "L0_gnn_W2l", "L0_gnn_W2r"]):
                    sp.dma_start(w_raw[:, n, :], a[name]).then_inc(w_in, 16)
                sp.wait_ge(vec_prep, BOUNDED)
                sp.dma_start(bounds_d.rearrange("n (b r) -> r n b", r=P), tile_bounds[:, :, :], allow_slow_non_contiguous=True).then_inc(bounds_out, 16)
                sp.wait_ge(bounds_out, 16)
                sp.dma_start(bounds.rearrange("p h c -> p (h c)"), bounds_d.rearrange("n c -> (n c)").rearrange("(o c) -> o c", o=1).broadcast_to([P, 2 * edge_cols])).then_inc(bounds_in, 16)
                for place, first, count in X_PLACES:
                    whole_tiles = min(count, NODE_TILES - 1 - first)
                    for t in range(0, whole_tiles, 4):
                        n = min(4, whole_tiles - t)
                        rows = a["x"][(first + t) * P:(first + t + n) * P, :].rearrange("(t p) f -> p t f", p=P)
                        sp.dma_start(place[:, t:t + n, :], rows).then_inc(x_in, 16)
                sp.dma_start(x_tile(NODE_TILES - 1)[0:LAST_NODES, :], a["x"][(NODE_TILES - 1) * P:N_NODES, :]).then_inc(x_in, 16)
                for n, name in enumerate(["L0_gnn_b1l", "L0_gnn_b2l"]):
                    sp.dma_start(bias[:, n:n + 1], a[name].rearrange("(p o) -> p o", o=1)).then_inc(small_in, 16)
                for f in range(2):
                    sp.dma_start(bias[:, 2 + f:3 + f], a["L1_gnn_b1"][f * P:(f + 1) * P].rearrange("(p o) -> p o", o=1)).then_inc(small_in, 16)
                for n, name in enumerate(["L1_gnn_b2", "L1_gnn_b3"]):
                    sp.dma_start(bias[:, 4 + n:5 + n], a[name].rearrange("(p o) -> p o", o=1)).then_inc(small_in, 16)
                sp.dma_start(emb[NTYPE, :], a["L1_gnn_node_emb"]).then_inc(small_in, 16)
                sp.dma_start(emb_T[:, 0, 0:NODE_TYPES], a["L1_gnn_node_emb"].rearrange("t p -> p t"), allow_slow_non_contiguous=True).then_inc(small_in, 16)
                sp.dma_start(root1[:, :, :], a["L1_gnn_root1"].rearrange("(h p) o -> p h o", p=P)).then_inc(small_in, 16)
                sp.dma_start(root2[:, :, :], a["L1_gnn_root2"].rearrange("(h p) o -> p h o", p=P)).then_inc(small_in, 16)
                sp.dma_start(root3[:, :], a["L1_gnn_root3"]).then_inc(small_in, 16)
                sp.wait_ge(padded, 5)
                sp.dma_start(ntype_i, a["node_type_3"].rearrange("(o n) -> o n", o=1).broadcast_to([NODE_TYPES, N_NODES])).then_inc(ntype_in, 16)

                def load_table_weights(p, name):
                    n = TABLE_COLS[p]
                    for h in range(WEIGHT_HALVES[p]):
                        sp.dma_start(table_w[:, h * n:(h + 1) * n].rearrange("p (r o) -> p r o", r=RELATIONS),
                                     a[name][:, h * P:(h + 1) * P, :].rearrange("r p o -> p r o")).then_inc(table_w_in, 16)

                sp.wait_ge(types_padded, 32)
                sp.wait_ge(prep_kept, len(FILLS))
                load_table_weights(1, "L1_gnn_W1")

                with sp.Fori(0, GROUPS) as g:
                    sp.wait_ge(etype_hot_ready, g)
                    sp.dma_start(etype_row, types_d[0:1, ds(g * (GROUP * P), GROUP * P)].broadcast_to([RELATIONS, GROUP * P])).then_inc(etype_in, 16)
                sp.wait_ge(table_psum[1], NODE_TILES * tile_copies(1))
                load_table_weights(2, "L1_gnn_W2")
                sp.wait_ge(table_psum[2], NODE_TILES * tile_copies(2))
                load_table_weights(3, "L1_gnn_W3")

                def store_out(c, tiles):
                    sp.wait_ge(normed_ready, c + (CHUNKS + 1))
                    rows = out[chunk_cols(c, tiles), :].rearrange("(t p) f -> p t f", p=P)
                    sp.dma_start(rows, normed[:, 0:tiles, :]).then_inc(out_stored, 16)

                with sp.Fori(0, FULL_CHUNKS) as c:
                    store_out(c, CHUNK_TILES)
                store_out(FULL_CHUNKS, LAST_CHUNKS[0])
                store_out(CHUNKS - 1, LAST_CHUNKS[1] - 1)
                sp.dma_start(out[(NODE_TILES - 1) * P:N_NODES, :], normed[0:LAST_NODES, LAST_CHUNKS[1] - 1, :]).then_inc(out_stored, 16)
                sp.wait_ge(out_stored, 16 * (CHUNKS + 1))

            @block.gpsimd
            def _(pool):
                pool.memset(edge_i[0][:, FULL_BLOCKS, :], NO_NODE).then_inc(padded, 1)
                pool.memset(edge_i[1][:, FULL_BLOCKS, :], 0).then_inc(padded, 1)
                pool.memset(edge_i[2][:, FULL_BLOCKS, :], 0).then_inc(padded, 1)
                pool.memset(x_tile(NODE_TILES - 1), 0.0).then_inc(padded, 1)
                pool.iota(iota_i[:, :], [[1, P]], base=0, channel_multiplier=0).then_inc(consts, 1)
                pool.iota(limit_i[:, 0:LAST_GROUPS.start], [[CHUNK, STRETCHES], [0, SLOTS]], base=0, channel_multiplier=0).then_inc(consts, 1)
                pool.iota(limit_i[:, LAST_GROUPS.start:GROUPS], [[0, len(LAST_GROUPS)]], base=LAST_FIRST * P, channel_multiplier=0).then_inc(consts, 1)
                for n, start in enumerate([0, NTYPE.start]):
                    pool.iota(lane_i[:, n:n + 1], [[0, 1]], base=-start, channel_multiplier=1).then_inc(consts, 1)
                pool.memset(ones[:, :], 1.0).then_inc(consts, 1)
                pool.memset(eps[:, :], EPS).then_inc(consts, 1)
                pool.memset(zeros[:, :], 0.0).then_inc(consts, 1)
                pool.memset(emb_T[:, 1:3, :], 0.0).then_inc(consts, 1)
                pool.memset(emb_T[:, 0, NODE_TYPES:BAND], 0.0).then_inc(consts, 1)
                pool.memset(S[3][:, :], 0.0).then_inc(padded, 1)

                for conv in range(CONVS):
                    width = CONV_WIDTH[conv]
                    if conv:
                        for s in range(2):
                            pool.wait_ge(row_stored[conv - 1][s], 16 * stores_in_all(s))
                    with pool.Fori(0, PAIRS) as i:
                        for half in range(2):
                            pool.wait_ge(cursor_ready, CURSORS * GROUPS * conv + i * (2 * CURSORS) + (CURSORS * half + 1))
                            pool.sem_inc(gathers_begun, 1)
                            for k in range(GROUP):
                                at = (half * GROUP + k) * width
                                pool.indirect_dma_start(
                                    msgs[:, at:at + width], None, GATHERED[conv],
                                    bass.IndirectOffsetOnAxis(ap=row_cur[:, half, k:k + 1], axis=0),
                                ).then_inc(gathered[half][k], 16)

            @block.scalar
            def _(act):
                def keep_turned(n):
                    what, at, count = FILLS[n]
                    act.wait_ge(prep_psum, n + 1)
                    src = bank[n % 8][:, 0:count * P]
                    if what == "w":
                        to = w_T[:, :, :].rearrange("p n f -> p (n f)")
                    elif what == "x":
                        to = S[0][:, at * P:(at + count) * P]
                    elif what == 0:
                        to = dst_T[:, at * P:(at + count) * P]
                    elif what == 1:
                        to = src_T[:, at * P:(at + count) * P]
                    else:
                        count_t = min(count * P, EDGE_TILES - at * P)
                        to, src = type_all[:, at * P:at * P + count_t], src[:, 0:count_t]
                    act.copy(to, src).then_inc(prep_kept, 1)

                def row_cursor(conv, i, half):
                    cols = ds(i * (2 * GROUP) + half * GROUP, GROUP)
                    act.wait_ge(cursor_free, i * 2 + (GROUPS * conv + half + 1))
                    act.copy(row_cur[:, half, :], row_all[:, cols]).then_inc(cursor_ready, 1)

                def edge_cursors(conv, i, half):
                    cols = ds(i * (2 * GROUP) + half * GROUP, GROUP)
                    if conv == 1:
                        act.copy(rel_cur[:, half, :], rel_all[:, cols]).then_inc(cursor_ready, 2)
                    else:
                        act.copy(rel_cur[:, half, :], rel_all[:, cols]).then_inc(cursor_ready, 1)
                        act.copy(weight_cur[:, half, :], type_all[:, cols]).then_inc(cursor_ready, 1)

                def group(conv, i, half):
                    row_cursor(conv, i, half)
                    edge_cursors(conv, i, half)

                for n in range(EDGE_FILLS):
                    keep_turned(n)
                act.wait_ge(vec_prep, ROWS_READY)
                row_cursor(0, 0, 0)
                act.wait_ge(vec_prep, VEC_PREPARED)
                edge_cursors(0, 0, 0)
                for n in range(EDGE_FILLS, len(FILLS)):
                    keep_turned(n)
                ordered = act.value_load(ordered_i[0:1, 0:1], min_val=0, max_val=1)

                def table_rows(p, c, t):
                    copies = tile_copies(p)
                    act.wait_ge(row_stored[p][t % 2], stored_before(c, t % 2) * 16 + 16 * (t // 2))
                    for n, (at, size) in enumerate(cuts(TABLE_COLS[p])):
                        act.wait_ge(table_psum[p], first_tile(c) * copies + (t * copies + n + 1))
                        act.copy(stage[:, t % 2, at:at + size], bank[TABLE_BANKS[(t * copies + n) % 2]][:, 0:size]).then_inc(table_copied[p], 1)
                    act.wait_ge(table_copied[p], first_tile(c) * copies + (t + 1) * copies)
                    act.dma_start(STORED[p][tile_rows(c, t), :], stage[:, t % 2, 0:TABLE_COLS[p]]).then_inc(row_stored[p][t % 2], 16)

                def chunk_slice(conv, c, at, tiles):
                    cols = chunk_cols(c, tiles)
                    if at == 0 and conv < 2:
                        act.wait_ge(inverted, c * 3 + 3)
                        act.copy(chunk_in[:, 1, 0:tiles * P], S[3][:, cols]).then_inc(counts_kept, 1)
                    if at == 1 and conv == 1:
                        act.wait_ge(counts_kept, c + (CHUNKS + 1))
                        act.wait_ge(table_psum[1], first_tile(c) * tile_copies(1))
                        for n in range(3):
                            act.copy(type_bands[n * BAND:(n + 1) * BAND, 0:tiles * P], chunk_in[NTYPE.start:NTYPE.start + BAND, 1, 0:tiles * P]).then_inc(chunk_kept[1], 1)
                    if at == UPDATE_AT[conv] + 1 and conv in (0, 2, 3):
                        act.wait_ge(updated[conv], c + 1)
                        for h, src in enumerate(TABLE_IN[conv]):
                            act.copy(chunk_in[:, h, 0:tiles * P], src[:, cols]).then_inc(chunk_kept[conv], 1)
                    if at == TURN_AT[conv] + 1 and conv in (1, 4):
                        seen = CHUNKS * (conv // 4)
                        act.wait_ge(norm_step, c * 3 + (seen * 3 + 2))
                        act.activation(rstd[:, 0:tiles], moments[:, 0:tiles, 1], ACT.Sqrt, bias=eps[:, 0:1]).then_inc(deviation, 1)
                    if at == TURN_AT[1] + 2 and conv == 1:
                        act.wait_ge(emb_psum, c + 1)
                        act.copy(S[1][:, cols], bank[EMB_BANK][:, 0:tiles * P]).then_inc(emb_kept, 1)
                        act.wait_ge(turned_back, c + 1)
                        act.copy(S[0][:, cols], bank[BACK_BANK][:, 0:tiles * P]).then_inc(norm_kept, 1)
                        act.copy(chunk_in[:, 0, 0:tiles * P], bank[BACK_BANK][:, 0:tiles * P]).then_inc(chunk_kept[1], 1)
                    if conv < 4:
                        for t in TILE_SLOTS[conv].get(at - 1, []):
                            if t < tiles:
                                table_rows(conv, c, t)

                def last_group(conv, g, may_be_wide):
                    if g + 1 < GROUPS:
                        group(conv, (g + 1) // 2, (g + 1) % 2)

                for conv in range(CONVS):
                    if conv:
                        group(conv, 0, 0)
                    with act.If(ordered):
                        with act.Fori(0, STRETCH_PAIRS) as i:
                            for half in range(2):
                                group(conv, i + half, 1 - half)
                        with act.Fori(1, STRETCHES) as o:
                            for slot in range(SLOTS):
                                group(conv, o * STRETCH_PAIRS + (slot + 1) // 2, (slot + 1) % 2)
                                if slot >= CHUNK_SLOT:
                                    chunk_slice(conv, o - 1, slot - CHUNK_SLOT, CHUNK_TILES)
                        for n, g in enumerate(LAST_GROUPS):
                            last_group(conv, g, False)
                            for at in range(2 * n, min(2 * n + 2, SLICES)):
                                chunk_slice(conv, FULL_CHUNKS, at, LAST_CHUNKS[0])
                    with act.Else():
                        with act.Fori(0, STRETCHES * STRETCH_PAIRS) as i:
                            for half in range(2):
                                group(conv, i + half, 1 - half)
                        for g in LAST_GROUPS:
                            last_group(conv, g, True)
                        with act.Fori(0, FULL_CHUNKS) as c:
                            for at in range(SLICES):
                                chunk_slice(conv, c, at, CHUNK_TILES)
                        for at in range(SLICES):
                            chunk_slice(conv, FULL_CHUNKS, at, LAST_CHUNKS[0])
                    for at in range(SLICES):
                        chunk_slice(conv, CHUNKS - 1, at, LAST_CHUNKS[1])

            @block.tensor
            def _(pe):
                pe.wait_ge(vec_prep, EDGES_IN_FLOAT)
                pe.wait_ge(w_in, 16 * 4)
                for n, (what, at, count) in enumerate(FILLS):
                    if n == EDGE_FILLS:
                        pe.wait_ge(x_in, 16 * X_LOADS)
                    if n >= 8:
                        pe.wait_ge(prep_kept, n - 7)
                    for m in range(count):
                        if what == "w":
                            block_in = w_raw[:, m, :]
                        elif what == "x":
                            block_in = x_tile(at + m)
                        else:
                            block_in = edge_f[what][:, at + m, :]
                        mm = pe.transpose(bank[n % 8][:, m * P:(m + 1) * P], block_in, ident[:, :])
                    mm.then_inc(prep_psum, 1)
                pe.wait_ge(prep_kept, len(FILLS))

                pe.wait_ge(vec_prep, VEC_PREPARED)
                wide = pe.value_load(wide_i[0:1, 0:1], min_val=0, max_val=1)
                ordered = pe.value_load(ordered_i[0:1, 0:1], min_val=0, max_val=1)

                def lookups(half, window, filled, used, reads):
                    for q in range(LOOKUP_FILLS):
                        if reads:
                            pe.wait_ge(used, reads[q])
                        pe.sem_inc(lookups_begun, 1)
                        for k in range(4 * q, min(4 * q + 4, GROUP)):
                            mm = pe.matmul(bank[LOOKUP_BANKS[q]][:, k % 4 * P:(k % 4 + 1) * P], etype_hot[:, half, k * P:(k + 1) * P],
                                           S[3][INVERSE, window], start=True, stop=True)
                        mm.then_inc(filled, 1)

                def prepare(conv, i, half):
                    if conv != 1:
                        return
                    g = i * 2 + half
                    base = pe.value_load(base_i[0:1, ds(g, 1)], min_val=0, max_val=N_NODES - 1)
                    pe.wait_ge(etype_hot_ready, g + 1)
                    first = isinstance(g, int) and g == 0
                    lookups(half, ds(base, P), lookup_psum, looked_up, None if first else [g * LOOKUP_FILLS + (q + 1 - LOOKUP_FILLS) for q in range(LOOKUP_FILLS)])

                def finish(conv, i, half, may_be_wide):
                    g = i * 2 + half
                    seen = GROUPS * conv
                    pe.wait_ge(cursor_free, g + (seen + 2))
                    pe.wait_ge(onehot_ready, g + (seen + 1))
                    for k in range(GROUP):
                        pe.wait_ge(gathered[half][k], i * 16 + 16 * (PAIRS * conv + 1))
                        for f in range(CONV_WIDTH[conv] // P):
                            mm = pe.matmul(bank[f][:, 0:P], message(conv, half, k, f), onehot[:, half, k, :],
                                           start=(k == 0), stop=(k == GROUP - 1))
                        if conv == 0:
                            mm = pe.matmul(bank[COUNT_BANK][0:32, 0:P], typehot[:, half, k, :], onehot[:, half, k, :],
                                           start=(k == 0), stop=(k == GROUP - 1))
                    mm.then_inc(sums_psum, 1)
                    if not may_be_wide:
                        return
                    with pe.If(wide):
                        with pe.Fori(1, WINDOWS) as j:
                            step = g * (WINDOWS - 1) + j
                            pe.wait_ge(wide_onehot, step + seen * (WINDOWS - 1))
                            if conv == 1:
                                lookups(half, ds(j * P, P), wide_lookup, wide_looked_up, [(step - 1) * LOOKUP_FILLS] * LOOKUP_FILLS)
                            for f in range(CONV_WIDTH[conv] // P):
                                for k in range(GROUP):
                                    mm = pe.matmul(bank[WIDE_BANK][:, f * P:(f + 1) * P], message(conv, half, k, f), onehot[:, half, k, :],
                                                   start=(k == 0), stop=(k == GROUP - 1))
                            if conv == 0:
                                for k in range(GROUP):
                                    mm = pe.matmul(bank[WIDE_BANK][0:32, 2 * P:3 * P], typehot[:, half, k, :], onehot[:, half, k, :],
                                                   start=(k == 0), stop=(k == GROUP - 1))
                            mm.then_inc(wide_psum, 1)

                def degrees(p, c, tiles):
                    seen = CHUNKS * p
                    pe.wait_ge(counts_kept, c + (seen + 1))
                    pe.wait_ge(scaled, c + seen)
                    if p == 1:
                        pe.wait_ge(table_copied[1], first_tile(c) * tile_copies(1))
                    pe.matmul(bank[DEGREE_BANK][:, 0:tiles * P], ones[COUNT, :], chunk_in[COUNT, 1, 0:tiles * P],
                              start=True, stop=True).then_inc(deg_psum, 1)

                def update(p, c, tiles):
                    pe.wait_ge(updated[p], c)
                    if p < 2:
                        pe.wait_ge(scaled, c + (CHUNKS * p + 1))
                    for f, terms in enumerate(UPDATE[p]):
                        for n, (w, src) in enumerate(terms):
                            mm = pe.matmul(bank[UPDATE_BANKS[p][f]][:, 0:tiles * P], w, src[:, chunk_cols(c, tiles)],
                                           start=(n == 0), stop=(n == len(terms) - 1))
                    mm.then_inc(update_psum[p], 1)

                def turn(p, c, tiles):
                    pe.wait_ge(updated[p], c + 1)
                    for t in range(tiles):
                        mm = pe.transpose(bank[TURN_BANK[p]][:, t * P:(t + 1) * P], chunk_in[:, 0, t * P:(t + 1) * P], ident[:, :])
                    mm.then_inc(turned, 1)

                def embed(c, tiles):
                    pe.matmul(bank[EMB_BANK][:, 0:tiles * P], emb[NTYPE, :], chunk_in[NTYPE, 1, 0:tiles * P],
                              start=True, stop=True).then_inc(emb_psum, 1)

                def turn_back(c, tiles):
                    pe.wait_ge(normed_ready, c + 1)
                    for t in range(tiles):
                        mm = pe.transpose(bank[BACK_BANK][:, t * P:(t + 1) * P], normed[:, t, :], ident[:, :])
                    mm.then_inc(turned_back, 1)

                def table(p, c, t):
                    copies = tile_copies(p)
                    pe.wait_ge(chunk_kept[p], c * chunk_copies(p) + chunk_copies(p))
                    if p == 1:
                        pe.wait_ge(norm_kept, c + 1)
                        pe.wait_ge(emb_kept, c + 1)
                        pe.wait_ge(emb_split, SPLIT_STEPS * len(EMB_BANKS))
                    if p:
                        pe.wait_ge(table_w_in, 16 * [0, 2, 4, 5][p])
                    for m, (at, size) in enumerate(cuts(TABLE_COLS[p])):
                        n = t * copies + m
                        pe.wait_ge(table_copied[p], first_tile(c) * copies + max(0, n - 1))
                        halves = len(TABLE_IN[p])
                        for h in range(halves):
                            mm = pe.matmul(bank[TABLE_BANKS[n % 2]][:, 0:size], chunk_in[:, h, t * P:(t + 1) * P], table_weights(p, h, at, size),
                                           start=(h == 0), stop=(p != 1 and h == halves - 1))
                        if p == 1:
                            mm = pe.matmul(bank[TABLE_BANKS[n % 2]][:, 0:size], type_bands[:, t * P:(t + 1) * P], emb_table[:, at:at + size],
                                           start=False, stop=True)
                        mm.then_inc(table_psum[p], 1)

                def chunk_slice(conv, c, at, tiles):
                    if at == 0:
                        if conv < 2:
                            degrees(conv, c, tiles)
                    if at == UPDATE_AT[conv]:
                        update(conv, c, tiles)
                    if at == TURN_AT[conv] and conv in (1, 4):
                        turn(conv, c, tiles)
                    if at == TURN_AT[1] and conv == 1:
                        embed(c, tiles)
                    if at == TURN_AT[1] + 1 and conv == 1:
                        turn_back(c, tiles)
                    if conv < 4:
                        for t in TILE_SLOTS[conv].get(at, []):
                            if t < tiles:
                                table(conv, c, t)

                def embedding_rows(cut):
                    at, size = cuts(TABLE_COLS[1])[cut]
                    pe.wait_ge(emb_split, SPLIT_STEPS * max(0, cut - 1))
                    pe.matmul(bank[EMB_BANKS[cut]][0:3 * BAND, 0:size], emb_T[:, :, :].rearrange("p n f -> p (n f)"), emb_weights[:, at:at + size],
                              start=True, stop=True).then_inc(emb_rows_psum, 1)

                pe.wait_ge(small_in, 16 * SMALL_LOADS)
                def last_group(conv, g, may_be_wide):
                    if g + 1 < GROUPS:
                        prepare(conv, (g + 1) // 2, (g + 1) % 2)
                    finish(conv, g // 2, g % 2, may_be_wide)
                    if conv == 0 and g == GROUPS - 3:
                        pe.wait_ge(emb_spread, 2)
                        pe.wait_ge(table_w_in, 32)
                        embedding_rows(0)
                        embedding_rows(1)
                    if conv == 0 and g == GROUPS - 1:
                        embedding_rows(2)
                        pe.wait_ge(emb_split, SPLIT_STEPS * 3)

                for conv in range(CONVS):
                    prepare(conv, 0, 0)
                    with pe.If(ordered):
                        with pe.Fori(0, STRETCH_PAIRS) as i:
                            for half in range(2):
                                prepare(conv, i + half, 1 - half)
                                finish(conv, i, half, False)
                        with pe.Fori(1, STRETCHES) as o:
                            for slot in range(SLOTS):
                                prepare(conv, o * STRETCH_PAIRS + (slot + 1) // 2, (slot + 1) % 2)
                                finish(conv, o * STRETCH_PAIRS + slot // 2, slot % 2, False)
                                if slot >= CHUNK_SLOT:
                                    chunk_slice(conv, o - 1, slot - CHUNK_SLOT, CHUNK_TILES)
                        for n, g in enumerate(LAST_GROUPS):
                            last_group(conv, g, False)
                            for at in range(2 * n, min(2 * n + 2, SLICES)):
                                chunk_slice(conv, FULL_CHUNKS, at, LAST_CHUNKS[0])
                    with pe.Else():
                        with pe.Fori(0, STRETCHES * STRETCH_PAIRS) as i:
                            for half in range(2):
                                prepare(conv, i + half, 1 - half)
                                finish(conv, i, half, True)
                        for g in LAST_GROUPS:
                            last_group(conv, g, True)
                        pe.wait_ge(cursor_free, freed(conv))
                        with pe.Fori(0, FULL_CHUNKS) as c:
                            for at in range(SLICES):
                                chunk_slice(conv, c, at, CHUNK_TILES)
                        for at in range(SLICES):
                            chunk_slice(conv, FULL_CHUNKS, at, LAST_CHUNKS[0])
                    for at in range(SLICES):
                        chunk_slice(conv, CHUNKS - 1, at, LAST_CHUNKS[1])

            @block.vector
            def _(vec):
                def step(op, n):
                    op.then_inc(vec_prep, 1)
                    vec.wait_ge(vec_prep, n)

                vec.wait_ge(consts, 8)
                step(vec.tensor_copy(iota_f[:, :], iota_i[:, :]), 1)
                step(vec.tensor_copy(lane_f[:, :], lane_i[:, :]), 2)
                step(vec.tensor_scalar(ident[:, :], iota_f[:, :], lane_f[:, 0:1], None, ALU.is_equal), 3)
                vec.wait_ge(dst_in, 48)
                step(vec.tensor_copy(edge_f[0], edge_i[0]), 4)
                step(vec.tensor_reduce(tile_bounds[:, 0, :], edge_f[0], AX.X, ALU.min), 5)
                step(vec.scalar_tensor_tensor(out=onehot[:, 0, :, :], in0=edge_f[0], scalar=float(NO_NODE), in1=edge_f[0], op0=ALU.is_lt, op1=ALU.mult), 6)
                step(vec.tensor_reduce(tile_bounds[:, 1, :], onehot[:, 0, :, :], AX.X, ALU.max), BOUNDED)
                vec.wait_ge(edges_in, 96)
                vec.wait_ge(types_padded, 32)
                step(vec.tensor_copy(edge_f[1], edge_i[1]), 8)
                step(vec.tensor_copy(edge_f[2], edge_i[2]), EDGES_IN_FLOAT)
                vec.wait_ge(prep_kept, EDGE_FILLS)
                step(vec.tensor_copy(row_all[:, :], src_T[:, 0:EDGE_TILES]), ROWS_READY)
                for n in range(2):
                    vec.sem_inc(cursor_free, 1)
                step(vec.tensor_copy(limit_f[:, :], limit_i[:, :]), 11)
                by_group = lambda v: v[:, 0:EDGE_TILES].rearrange("p (g k) -> p g k", k=GROUP)
                vec.wait_ge(bounds_in, 16)
                step(vec.tensor_reduce(base_f[:, :], by_group(bounds[:, 0, :]), AX.X, ALU.min), 12)
                step(vec.tensor_reduce(high_f[:, :], by_group(bounds[:, 1, :]), AX.X, ALU.max), 13)
                for to, groups in [(slice(0, LAST_GROUPS.start), slice(CHUNK_SLOT, CHUNK_SLOT + LAST_GROUPS.start)),
                                   (slice(LAST_GROUPS.start, GROUPS), slice(LAST_GROUPS.start, GROUPS))]:
                    op = vec.tensor_tensor(limit_f[:, to], base_f[:, groups], limit_f[:, to], ALU.subtract)
                step(op, 14)
                step(vec.tensor_reduce(ordered_f[:, :], limit_f[:, :], AX.X, ALU.min), 15)
                step(vec.tensor_tensor(span_f[:, :], high_f[:, :], base_f[:, :], ALU.subtract), 16)
                step(vec.tensor_reduce(wide_f[:, :], span_f[:, :], AX.X, ALU.max), 17)
                step(vec.tensor_scalar(wide_f[:, :], wide_f[:, :], float(P - 1), None, ALU.is_gt), 18)
                step(vec.tensor_scalar(narrow_f[:, :], wide_f[:, :], -1.0, 1.0, ALU.mult, ALU.add), 19)
                step(vec.tensor_scalar(ordered_f[:, :], ordered_f[:, :], 0.0, narrow_f[:, 0:1], ALU.is_ge, ALU.mult), 20)
                step(vec.tensor_scalar(base_f[:, :], base_f[:, :], narrow_f[:, 0:1], None, ALU.mult), 21)
                step(vec.tensor_copy(base_i[:, :], base_f[0:1, :]), 22)
                step(vec.tensor_copy(wide_i[:, :], wide_f[0:1, :]), 23)
                step(vec.tensor_copy(ordered_i[:, :], ordered_f[0:1, :]), 24)
                step(vec.tensor_tensor(by_group(rel_all), by_group(dst_T), base_f[:, :].unsqueeze(2).broadcast_to([P, GROUPS, GROUP]), ALU.subtract), VEC_PREPARED)

                ordered = vec.value_load(ordered_i[0:1, 0:1], min_val=0, max_val=1)
                wide = vec.value_load(wide_i[0:1, 0:1], min_val=0, max_val=1)

                def build_onehots(conv, half, rel, signal):
                    for k in range(GROUP):
                        weight = dict(scalar2=weight_cur[:, half, k:k + 1], op1=ALU.mult) if conv >= 2 else dict(scalar2=None)
                        op = vec.tensor_scalar(onehot[:, half, k, :], iota_f[:, :], scalar1=rel(k), op0=ALU.is_equal, **weight)
                    op.then_inc(signal, 1)

                def add_sums(conv, source, window):
                    for f, sums in enumerate(SUMS[conv]):
                        op = vec.tensor_tensor(sums[:, window], sums[:, window], source[f], ALU.add)
                    if conv == 0:
                        op = vec.tensor_tensor(S[3][SUMMED, window], S[3][SUMMED, window], source[-1], ALU.add)
                    return op

                def lookups(half, into, seen, filled, used):
                    for q in range(LOOKUP_FILLS):
                        vec.wait_ge(filled, seen + (q + 1))
                        for k in range(4 * q, min(4 * q + 4, GROUP)):
                            at = bank[LOOKUP_BANKS[q]][:, k % 4 * P:(k % 4 + 1) * P]
                            op = vec.tensor_tensor_reduce(at, at, onehot[:, half, k, :], 1.0, 0.0, ALU.mult, ALU.add, into[:, k:k + 1])
                        op.then_inc(used, 1)

                def type_onehots(i, half):
                    g = i * 2 + half
                    vec.wait_ge(etype_in, g * 16 + 16)
                    vec.tensor_scalar(etype_hot[:, half, :], etype_row, lane_f[INVERSE, 0:1], None, ALU.is_equal).then_inc(etype_hot_ready, 1)

                def prepare(conv, i, half):
                    g = i * 2 + half
                    seen = GROUPS * conv
                    vec.wait_ge(cursor_ready, g * CURSORS + CURSORS * (seen + 1))
                    if conv == 0:
                        vec.tensor_tensor(typehot[:, half, :, :], iota_f[:, 0:32].unsqueeze(1).broadcast_to([P, GROUP, 32]),
                                          weight_cur[:, half, :].unsqueeze(2).broadcast_to([P, GROUP, 32]), ALU.is_equal)
                    build_onehots(conv, half, lambda k: rel_cur[:, half, k:k + 1], onehot_ready)
                    if conv == 1:
                        vec.wait_ge(onehot_ready, g + (seen + 1))
                        lookups(half, part[:, half, :], g * LOOKUP_FILLS, lookup_psum, looked_up)

                def finish(conv, i, half, may_be_wide):
                    g = i * 2 + half
                    seen = GROUPS * conv
                    base = vec.value_load(base_i[0:1, ds(g, 1)], min_val=0, max_val=N_NODES - 1)
                    if may_be_wide:
                        with vec.If(wide):
                            wide_windows(conv, g, half, seen)
                    if conv == 1:
                        vec.wait_ge(looked_up, g * LOOKUP_FILLS + LOOKUP_FILLS)
                        rows, types = row_all[:, ds(g * GROUP, GROUP)], type_all[:, ds(g * GROUP, GROUP)]
                        vec.scalar_tensor_tensor(out=rows, in0=rows, scalar=float(RELATIONS), in1=types, op0=ALU.mult, op1=ALU.add).then_inc(rel_rows_made, 1)
                        vec.wait_ge(rel_rows_made, g + 1)
                        vec.sem_inc(weighed, 1)
                        vec.tensor_copy(weight_all[:, ds(g * GROUP, GROUP)], part[:, half, :])
                    vec.wait_ge(sums_psum, g + (seen + 1))
                    source = [bank[f][:, 0:P] for f in range(CONV_WIDTH[conv] // P)] + [bank[COUNT_BANK][0:32, 0:P]]
                    add_sums(conv, source, ds(base, P)).then_inc(cursor_free, 1)
                    vec.wait_ge(cursor_free, g + (seen + 3))

                def wide_windows(conv, g, half, seen):
                    vec.wait_ge(sums_psum, g + (seen + 1))
                    if conv == 1:
                        vec.wait_ge(looked_up, g * LOOKUP_FILLS + LOOKUP_FILLS)
                    rel_steps = WINDOWS
                    vec.tensor_copy(rel_wide[:, :], rel_cur[:, half, :]).then_inc(wide_rel, 1)
                    with vec.Fori(1, WINDOWS) as j:
                        in_conv = g * (WINDOWS - 1) + j
                        done = in_conv + seen * (WINDOWS - 1)
                        vec.wait_ge(wide_rel, g * rel_steps + j + seen * rel_steps)
                        vec.tensor_scalar(rel_wide[:, :], rel_wide[:, :], -float(P), None, ALU.add).then_inc(wide_rel, 1)
                        vec.wait_ge(wide_rel, g * rel_steps + j + (seen * rel_steps + 1))
                        build_onehots(conv, half, lambda k: rel_wide[:, k:k + 1], wide_onehot)
                        vec.wait_ge(wide_onehot, done)
                        if conv == 1:
                            lookups(half, part_wide, (in_conv - 1) * LOOKUP_FILLS, wide_lookup, wide_looked_up)
                            vec.wait_ge(wide_looked_up, in_conv * LOOKUP_FILLS)
                            vec.tensor_tensor(part[:, half, :], part[:, half, :], part_wide[:, :], ALU.add).then_inc(wide_part, 1)
                            vec.wait_ge(wide_part, in_conv)
                        vec.wait_ge(wide_psum, done)
                        source = [bank[WIDE_BANK][:, f * P:(f + 1) * P] for f in range(CONV_WIDTH[conv] // P)] + [bank[WIDE_BANK][0:32, 2 * P:3 * P]]
                        add_sums(conv, source, ds(j * P, P))

                def invert_counts(c, tiles):
                    cols = chunk_cols(c, tiles)
                    vec.tensor_copy(S[3][COUNT, cols], S[3][SUMMED, cols]).then_inc(inverted, 1)
                    vec.wait_ge(inverted, c * 3 + 1)
                    vec.tensor_scalar(S[3][INVERSE, cols], S[3][INVERSE, cols], 1.0, None, ALU.max).then_inc(inverted, 1)
                    vec.wait_ge(inverted, c * 3 + 2)
                    vec.sem_inc(inverting, 1)
                    vec.reciprocal(S[3][INVERSE, cols], S[3][INVERSE, cols]).then_inc(inverted, 1)

                def scale_by_degree(p, c, tiles):
                    seen = CHUNKS * p
                    inv = inv_deg[:, 0:tiles * P]
                    vec.wait_ge(deg_psum, c + (seen + 1))
                    vec.tensor_scalar(inv, bank[DEGREE_BANK][:, 0:tiles * P], 1.0, None, ALU.max).then_inc(deg_step, 1)
                    vec.wait_ge(deg_step, c * 2 + (2 * seen + 1))
                    vec.reciprocal(inv, inv).then_inc(deg_step, 1)
                    vec.wait_ge(deg_step, c * 2 + (2 * seen + 2))
                    sums = S[1 + p][:, chunk_cols(c, tiles)]
                    vec.tensor_tensor(sums, sums, inv, ALU.mult).then_inc(scaled, 1)

                def update(p, c, tiles):
                    cols = chunk_cols(c, tiles)
                    psum = [bank[b][:, 0:tiles * P] for b in UPDATE_BANKS[p]]
                    vec.wait_ge(update_psum[p], c + 1)
                    if p == 0:
                        vec.tensor_scalar(S[1][:, cols], psum[0], BIAS[0][0], 0.0, ALU.add, ALU.max).then_inc(updated[p], 1)
                        return
                    if p == 1:
                        vec.wait_ge(scaled, c + (CHUNKS + 1))
                    for f, sums in enumerate(SUMS[p]):
                        op = vec.scalar_tensor_tensor(out=sums[:, cols], in0=psum[f], scalar=BIAS[p][f], in1=sums[:, cols], op0=ALU.add, op1=ALU.add)
                    op.then_inc(update_step[p], 1)
                    vec.wait_ge(update_step[p], c + 1)
                    if p == 1:
                        vec.wait_ge(table_psum[1], first_tile(c) * tile_copies(1))
                    fixed = chunk_in[:, 0, 0:tiles * P]
                    for f, sums in enumerate(SUMS[p]):
                        if p == 1:
                            op = vec.tensor_tensor(fixed, sums[:, cols], S[0][:, cols], ALU.add)
                        elif p == 4:
                            op = vec.scalar_tensor_tensor(out=fixed, in0=sums[:, cols], scalar=0.0, in1=S[0][:, cols], op0=ALU.max, op1=ALU.add)
                        else:
                            op = vec.tensor_scalar(sums[:, cols], sums[:, cols], 0.0, None, ALU.max)
                    op.then_inc(updated[p], 1)

                def norm(which, c, tiles):
                    seen = CHUNKS * which
                    source = bank[TURN_BANK[(1, 4)[which]]]
                    vec.wait_ge(turned, c + (seen + 1))
                    for t in range(tiles):
                        op = vec.bn_stats(stats[:, t, :], source[:, t * P:(t + 1) * P])
                    op.then_inc(norm_step, 1)
                    vec.wait_ge(norm_step, c * 3 + (seen * 3 + 1))
                    vec.sem_inc(moments_begun, 1)
                    for t in range(tiles):
                        op = vec.bn_aggr(moments[:, t, :], stats[:, t, :])
                    op.then_inc(norm_step, 1)
                    vec.wait_ge(deviation, c + (seen + 1))
                    vec.reciprocal(rstd[:, 0:tiles], rstd[:, 0:tiles]).then_inc(norm_step, 1)
                    vec.wait_ge(norm_step, c * 3 + (seen * 3 + 3))
                    if which == 0:
                        vec.wait_ge(turned_back, c)
                    else:
                        vec.wait_ge(out_stored, c * 16)
                    for t in range(tiles):
                        op = vec.tensor_scalar(normed[:, t, :], source[:, t * P:(t + 1) * P], moments[:, t, 0:1], rstd[:, t:t + 1], ALU.subtract, ALU.mult)
                    op.then_inc(normed_ready, 1)

                def zero(p, c, tiles):
                    width = ACC_COLS - LAST_FIRST * P if is_last(c) else tiles * P
                    if p == 1:
                        vec.wait_ge(updated[1], c + 1)
                        vec.wait_ge(counts_kept, c + (CHUNKS + 1))
                    vec.sem_inc(zeroing, 1)
                    for s in SUMS[p + 1]:
                        place = s[:, ds(first_tile(c) * P, width)]
                        op = vec.tensor_copy(place, zeros[:, 0:1].broadcast_to([P, width]))
                    op.then_inc(zeroed, 1)

                def split_embedding_rows(cut):
                    at, size = cuts(TABLE_COLS[1])[cut]
                    rows = lambda n, count=1: slice(n * BAND, (n + count) * BAND)
                    whole = lambda n, count=1: bank[EMB_BANKS[cut]][rows(n, count), 0:size]
                    kept = lambda n, count=1: emb_table[rows(n, count), at:at + size]
                    done = SPLIT_STEPS * cut
                    vec.wait_ge(emb_rows_psum, cut + 1)
                    vec.tensor_copy(kept(0, 3), whole(0, 3)).then_inc(emb_split, 1)
                    vec.wait_ge(emb_split, done + 1)
                    for n in (1, 2):
                        vec.tensor_tensor(whole(n), whole(n), kept(n), ALU.subtract).then_inc(emb_split, 1)
                    vec.wait_ge(emb_split, done + 3)
                    for n in (1, 2):
                        vec.tensor_copy(kept(n), whole(n)).then_inc(emb_split, 1)
                    vec.wait_ge(emb_split, done + 5)
                    vec.tensor_tensor(whole(2), whole(2), kept(2), ALU.subtract).then_inc(emb_split, 1)
                    vec.wait_ge(emb_split, done + 6)
                    vec.tensor_copy(kept(2), whole(2)).then_inc(emb_split, 1)

                def chunk_slice(conv, c, at, tiles):
                    if at == 0:
                        if conv == 0:
                            invert_counts(c, tiles)
                        if conv < 2:
                            scale_by_degree(conv, c, tiles)
                    if at == UPDATE_AT[conv]:
                        update(conv, c, tiles)
                        if conv <= 3:
                            zero(conv, c, tiles)
                    if at == TURN_AT[conv] and conv in (1, 4):
                        norm(conv // 4, c, tiles)

                def one_group(conv, i, half, may_be_wide):
                    following = [i * 2 + half + n < GROUPS if isinstance(i, int) else True for n in (1, 2)]
                    if following[0]:
                        prepare(conv, i + half, 1 - half)
                    types_follow = conv == 1 and following[1]
                    if types_follow and not may_be_wide:
                        type_onehots(i + 1, half)
                    finish(conv, i, half, may_be_wide)
                    if types_follow and may_be_wide:
                        type_onehots(i + 1, half)

                def last_group(conv, g, may_be_wide):
                    one_group(conv, g // 2, g % 2, may_be_wide)
                    if conv == 0 and g == GROUPS - 2:
                        split_embedding_rows(0)
                        split_embedding_rows(1)
                    if conv == 0 and g == GROUPS - 1:
                        split_embedding_rows(2)

                for conv in range(CONVS):
                    if conv:
                        vec.wait_ge(zeroed, CHUNKS * conv)
                    if conv == 1:
                        for half in range(2):
                            type_onehots(0, half)
                    prepare(conv, 0, 0)
                    if conv == 0:
                        step(vec.memset(S[1][:, :], 0.0), VEC_PREPARED + 1)
                        vec.wait_ge(ntype_in, 16)
                        step(vec.tensor_scalar(S[3][NTYPE, 0:N_NODES], ntype_i, lane_f[NTYPE, 1:2], None, ALU.is_equal), VEC_PREPARED + 2)
                        vec.wait_ge(small_in, 16 * SMALL_LOADS)
                        vec.wait_ge(consts, 10)
                        for n in range(1, 3):
                            vec.tensor_copy(emb_T[:, n, 0:NODE_TYPES], emb_T[:, 0, 0:NODE_TYPES]).then_inc(emb_spread, 1)
                    with vec.If(ordered):
                        with vec.Fori(0, STRETCH_PAIRS) as i:
                            for half in range(2):
                                one_group(conv, i, half, False)
                        with vec.Fori(1, STRETCHES) as o:
                            for slot in range(SLOTS):
                                one_group(conv, o * STRETCH_PAIRS + slot // 2, slot % 2, False)
                                if slot >= CHUNK_SLOT:
                                    chunk_slice(conv, o - 1, slot - CHUNK_SLOT, CHUNK_TILES)
                        for n, g in enumerate(LAST_GROUPS):
                            last_group(conv, g, False)
                            for at in range(2 * n, min(2 * n + 2, SLICES)):
                                chunk_slice(conv, FULL_CHUNKS, at, LAST_CHUNKS[0])
                    with vec.Else():
                        with vec.Fori(0, STRETCHES * STRETCH_PAIRS) as i:
                            for half in range(2):
                                one_group(conv, i, half, True)
                        for g in LAST_GROUPS:
                            last_group(conv, g, True)
                        with vec.Fori(0, FULL_CHUNKS) as c:
                            for at in range(SLICES):
                                chunk_slice(conv, c, at, CHUNK_TILES)
                        for at in range(SLICES):
                            chunk_slice(conv, FULL_CHUNKS, at, LAST_CHUNKS[0])
                    for at in range(SLICES):
                        chunk_slice(conv, CHUNKS - 1, at, LAST_CHUNKS[1])


_INS = ['x', 'src', 'dst', 'edge_type_5', 'node_type_3', 'L0_gnn_W1l', 'L0_gnn_b1l', 'L0_gnn_W1r', 'L0_gnn_W2l', 'L0_gnn_b2l',
        'L0_gnn_W2r', 'L1_gnn_node_emb', 'L1_gnn_W1', 'L1_gnn_root1', 'L1_gnn_b1', 'L1_gnn_W2', 'L1_gnn_root2', 'L1_gnn_b2',
        'L1_gnn_W3', 'L1_gnn_root3', 'L1_gnn_b3']


def kernel(**inputs):
    import numpy as np
    import concourse.bacc as bacc
    from concourse import mybir as mb
    from concourse.bass_utils import run_bass_kernel_spmd as run

    nc = bacc.Bacc("TRN2", target_bir_lowering=False, num_devices=1)
    arrays, aps = {}, {}
    for name in _INS:
        v = np.ascontiguousarray(inputs[name])
        arrays[f"in_{name}"] = v
        aps[name] = nc.dram_tensor(f"in_{name}", v.shape, mb.dt.from_np(v.dtype), kind="ExternalInput").ap()
    out = nc.dram_tensor("out", (N_NODES, FEAT), mb.dt.float32, kind="ExternalOutput").ap()
    resnorm_gnn(nc, aps, out)
    return run(nc, [arrays], core_ids=[0]).results[0]["out"]
```
